# Optimizing a Trainium2 kernel written in Bass

```python
import numpy as np
import jax
import jax.numpy as jnp

def _softmax(x, axis=-1):
    return jax.nn.softmax(x, axis=axis)
def _gelu(x):
    return jax.nn.gelu(x, approximate=True)
def _silu(x):
    return jax.nn.silu(x)
def _sigmoid(x):
    return jax.nn.sigmoid(x)
def _layernorm(x, axis=-1, eps=1e-5):
    m = jnp.mean(x, axis=axis, keepdims=True)
    v = jnp.var(x, axis=axis, keepdims=True)
    return (x - m) / jnp.sqrt(v + eps)
def _scatter_add(tgt, idx, src, axis=0):
    return tgt.at[idx].add(src)
def _segment_sum(src, seg, n):
    return jax.ops.segment_sum(src, seg, n)

kernel_name = 'mk_conv_seq_d2_conv_nchw64_fddb1f'

def setup_inputs(seed: int = 0):
    np.random.seed(seed)
    _w = jnp.asarray
    def _rec_inputs():
        import jax
        import jax.numpy as jnp
        _gk = jax.random.key(seed)
        x = -0.0003929 + 0.9999 * jax.random.normal(jax.random.fold_in(_gk, 1), (16, 64, 128, 128), jnp.float32)
        return x
    x = _rec_inputs()
    def _L0_conv_setup():
        import jax, jax.numpy as jnp
        import numpy as np
        from jax import lax
        CUTOFF = 0.25
        SIGMA = 1.0
        RADIUS = 4

        def _gauss_kernel(sigma=SIGMA, radius=RADIUS):
            x = np.arange(-radius, radius + 1, dtype=np.float32)
            k = np.exp(-0.5 * (x / sigma) ** 2)
            return jnp.asarray(k / k.sum())

        def _blur_axis(x, axis, kernel):
            r = (kernel.shape[0] - 1) // 2
            pad = [(0, 0)] * x.ndim
            pad[axis] = (r, r)
            xp = jnp.pad(x, pad, mode='edge')
            out = jnp.zeros_like(x)
            for i in range(kernel.shape[0]):
                out = out + kernel[i] * lax.slice_in_dim(xp, i, i + x.shape[axis], axis=axis)
            return out

        def gaussian_smoothing_4d(x):
            k = _gauss_kernel().astype(x.dtype)
            for ax in range(4):
                x = _blur_axis(x, ax, k)
            return x

        def dht_2d(x):
            return (jnp.fft.fftn(x, axes=(2, 3)).real - jnp.fft.fftn(jnp.flip(x, axis=(2, 3)), axes=(2, 3)).imag).astype(x.dtype)

        def _neg_k(a):
            return jnp.roll(jnp.flip(a, axis=(-2, -1)), shift=(1, 1), axis=(-2, -1))

        def compl_mul2d(x1, x2):
            x1n, x2n = (_neg_k(x1), _neg_k(x2))
            e = lambda a, b: jnp.einsum('bixy,ioxy->boxy', a, b)
            return 0.5 * (e(x1, x2) - e(x1n, x2n) + e(x1, x2n) + e(x1n, x2))
        key = jax.random.key(seed)
        k1, k2 = jax.random.split(key)
        B, Cin, Cout, H, W, M1, M2 = (16, 64, 64, 128, 128, 20, 20)
        x = jax.random.normal(k1, (B, Cin, H, W), dtype=jnp.float32)
        scale = 1.0 / (Cin * Cout)
        w1 = scale * jax.random.uniform(k2, (Cin, Cout, M1, M2), dtype=jnp.float32)
        return {'x': x, 'w1': w1}
    _L0_conv_all = _L0_conv_setup()
    _L0_conv_in = {k: v for k, v in _L0_conv_all.items() if k in ('w1', )}
    del _L0_conv_all

    def _L1_conv_setup():
        import jax, jax.numpy as jnp
        import numpy as np
        from jax import lax
        P = 8
        DN = ('NCHW', 'OIHW', 'NCHW')
        key = jax.random.key(seed)
        ks = jax.random.split(key, 8)
        B, D, H, W = (8, 64, 256, 256)
        C = 4 * D
        return {'x': jax.random.normal(ks[0], (B, D, H, W), jnp.float32), 'w_in': jax.random.normal(ks[1], (C, D, 1, 1), jnp.float32) * 0.05, 'b_in': jax.random.normal(ks[2], (C,), jnp.float32) * 0.05, 'fft_filter': jnp.ones((C, 1, 1, P, P // 2 + 1), jnp.float32), 'w_dw': jax.random.normal(ks[3], (C, 1, 7, 7), jnp.float32) * 0.05, 'b_dw': jax.random.normal(ks[4], (C,), jnp.float32) * 0.05, 'w_out': jax.random.normal(ks[5], (D, C, 1, 1), jnp.float32) * 0.05, 'b_out': jax.random.normal(ks[6], (D,), jnp.float32) * 0.05}
    _L1_conv_all = _L1_conv_setup()
    _L1_conv_in = {k: v for k, v in _L1_conv_all.items() if k in ('w_in', 'b_in', 'fft_filter', 'w_dw', 'b_dw', 'w_out', 'b_out', )}
    del _L1_conv_all

    return {
        "x": x,
        "L0_conv_w1": _L0_conv_in["w1"],
        "L1_conv_w_in": _L1_conv_in["w_in"],
        "L1_conv_b_in": _L1_conv_in["b_in"],
        "L1_conv_fft_filter": _L1_conv_in["fft_filter"],
        "L1_conv_w_dw": _L1_conv_in["w_dw"],
        "L1_conv_b_dw": _L1_conv_in["b_dw"],
        "L1_conv_w_out": _L1_conv_in["w_out"],
        "L1_conv_b_out": _L1_conv_in["b_out"],
    }

def reference(x, L0_conv_w1, L1_conv_w_in, L1_conv_b_in, L1_conv_fft_filter, L1_conv_w_dw, L1_conv_b_dw, L1_conv_w_out, L1_conv_b_out):
    import jax
    import jax.numpy as jnp
    def _L0_conv_ref(x, w1):
        import jax, jax.numpy as jnp
        import numpy as np
        from jax import lax
        CUTOFF = 0.25
        SIGMA = 1.0
        RADIUS = 4

        def _gauss_kernel(sigma=SIGMA, radius=RADIUS):
            x = np.arange(-radius, radius + 1, dtype=np.float32)
            k = np.exp(-0.5 * (x / sigma) ** 2)
            return jnp.asarray(k / k.sum())

        def _blur_axis(x, axis, kernel):
            r = (kernel.shape[0] - 1) // 2
            pad = [(0, 0)] * x.ndim
            pad[axis] = (r, r)
            xp = jnp.pad(x, pad, mode='edge')
            out = jnp.zeros_like(x)
            for i in range(kernel.shape[0]):
                out = out + kernel[i] * lax.slice_in_dim(xp, i, i + x.shape[axis], axis=axis)
            return out

        def gaussian_smoothing_4d(x):
            k = _gauss_kernel().astype(x.dtype)
            for ax in range(4):
                x = _blur_axis(x, ax, k)
            return x

        def dht_2d(x):
            return (jnp.fft.fftn(x, axes=(2, 3)).real - jnp.fft.fftn(jnp.flip(x, axis=(2, 3)), axes=(2, 3)).imag).astype(x.dtype)

        def _neg_k(a):
            return jnp.roll(jnp.flip(a, axis=(-2, -1)), shift=(1, 1), axis=(-2, -1))

        def compl_mul2d(x1, x2):
            x1n, x2n = (_neg_k(x1), _neg_k(x2))
            e = lambda a, b: jnp.einsum('bixy,ioxy->boxy', a, b)
            return 0.5 * (e(x1, x2) - e(x1n, x2n) + e(x1, x2n) + e(x1n, x2))
        B, _, H, W = x.shape
        Cout, M1, M2 = (w1.shape[1], w1.shape[2], w1.shape[3])
        x_ht = dht_2d(x)
        out_ht = jnp.zeros((B, Cout, H, W), dtype=x.dtype)
        out_ht = out_ht.at[:, :, :M1, :M2].set(compl_mul2d(x_ht[:, :, :M1, :M2], w1))
        y = dht_2d(out_ht) / (H * W)
        y = gaussian_smoothing_4d(y)
        freqs = jnp.fft.fftfreq(W)
        mask = (jnp.abs(freqs) <= CUTOFF).astype(y.dtype)
        return y * mask

    def _L1_conv_ref(x, w_in, b_in, fft_filter, w_dw, b_dw, w_out, b_out):
        import jax, jax.numpy as jnp
        import numpy as np
        from jax import lax
        P = 8
        DN = ('NCHW', 'OIHW', 'NCHW')
        B, D, H, W = x.shape
        C = w_in.shape[0]
        x = lax.conv_general_dilated(x, w_in, (1, 1), 'SAME', dimension_numbers=DN)
        x = x + b_in[None, :, None, None]
        xp = x.reshape(B, C, H // P, P, W // P, P).transpose(0, 1, 2, 4, 3, 5)
        xf = jnp.fft.rfft2(xp)
        xf = xf * fft_filter
        xp = jnp.fft.irfft2(xf, s=(P, P))
        x = xp.transpose(0, 1, 2, 4, 3, 5).reshape(B, C, H, W)
        x = lax.conv_general_dilated(x, w_dw, (1, 1), 'SAME', dimension_numbers=DN, feature_group_count=C)
        x = x + b_dw[None, :, None, None]
        x = jax.nn.gelu(x, approximate=False)
        x = lax.conv_general_dilated(x, w_out, (1, 1), 'SAME', dimension_numbers=DN)
        return x + b_out[None, :, None, None]

    def _gn(v, G=32, eps=1e-5):
        B_, C_, H_, W_ = v.shape
        g = v.reshape(B_, G, C_ // G, H_, W_)
        m = jnp.mean(g, axis=(2, 3, 4), keepdims=True)
        s = jnp.var(g, axis=(2, 3, 4), keepdims=True)
        return ((g - m) / jnp.sqrt(s + eps)).reshape(v.shape)

    def _ln_c(v, eps=1e-6):
        m = jnp.mean(v, axis=1, keepdims=True)
        s = jnp.var(v, axis=1, keepdims=True)
        return (v - m) / jnp.sqrt(s + eps)

    def _ln_t(v, eps=1e-5):
        m = jnp.mean(v, axis=-1, keepdims=True)
        s = jnp.var(v, axis=-1, keepdims=True)
        return (v - m) / jnp.sqrt(s + eps)

    def _to_tokens(v):
        B_, C_, H_, W_ = v.shape
        return v.reshape(B_, C_, H_ * W_).transpose(0, 2, 1)
    def _from_tokens(t, like):
        B_, C_, H_, W_ = like.shape
        return t.transpose(0, 2, 1).reshape(B_, C_, H_, W_)

    x = _L0_conv_ref(x, L0_conv_w1)
    x = _L1_conv_ref(x, L1_conv_w_in, L1_conv_b_in, L1_conv_fft_filter, L1_conv_w_dw, L1_conv_b_dw, L1_conv_w_out, L1_conv_b_out)
    return x


_drawn_inputs = setup_inputs


def setup_inputs(seed=0):
    import zlib

    import numpy as np

    out = dict(_drawn_inputs(seed))
    spreads = {'L1_conv_fft_filter': (1.0, 0.6)}
    factors = {'x': 25.245, 'L0_conv_w1': 64.0, 'L1_conv_w_in': 26.066}
    for name, (base, spread) in spreads.items():
        noise = np.random.default_rng([zlib.crc32(name.encode()), seed]).standard_normal(out[name].shape)
        drawn = base * np.exp(spread * noise) if base else spread * noise
        out[name] = jnp.asarray(drawn.astype(out[name].dtype))
    for name, factor in factors.items():
        out[name] = (out[name] * factor).astype(out[name].dtype)
    return out
```

```python
from contextlib import ExitStack

import concourse.bass as bass
from concourse import mybir

F32 = mybir.dt.float32
ACT = mybir.ActivationFunctionType
ALU = mybir.AluOpType

B, CI, H, W = 16, 64, 128, 128
C = 256
CH = C // 128
MODES = 20
NM = MODES * MODES
KC, KP = 4, NM // 4
P = 8
PF = P * P
NJ = H // (2 * P)
R = 4
TAPS = 7
LIVE = [0, 1, 2, 3, 4, 12, 13, 14, 15]
SLOT = [0, 1, 2, 3, 4, 7, 8, 9, 10]
CONST0, NCONST = 5, 2
NS = len(LIVE) + NCONST
NT = NS + 1
NX = NS * NJ
NZ = NT * NJ
CB = 4
NFAST = 96
MID0, MID1 = 44, 92


def constants():
    import numpy as np
    th = 2 * np.pi / W
    t = np.arange(-R, R + 1, dtype=np.float32)
    g = np.exp(-0.5 * t ** 2)
    g = (g / g.sum()).astype(np.float64)

    def smooth(n):
        m = np.zeros((n, n))
        for i in range(n):
            for k in range(2 * R + 1):
                m[i, min(max(i + k - R, 0), n - 1)] += g[k]
        return m

    u = np.arange(MODES)
    p = np.arange(H)
    c0, s0 = np.cos(th * np.outer(p, u)), np.sin(th * np.outer(p, u))
    c1, s1 = np.cos(th * np.outer(p + 1, u)), np.sin(th * np.outer(p + 1, u))
    basis_h = np.concatenate([c0, s0, c1, s1, np.zeros((H, NFAST - 4 * MODES))], 1)
    basis_w = np.stack([c0, -s0, -s1, -c1], 1)
    ident = np.eye(128)
    neg = np.zeros((MODES, MODES))
    neg[(-u) % MODES, u] = 1.0
    flip = np.concatenate([np.eye(MODES), np.eye(MODES), neg, -neg], 1)
    sm_c = smooth(CI).T
    sh = smooth(H)
    mask = (np.abs(np.fft.fftfreq(W)) <= 0.25).astype(np.float64)
    sw = mask[:, None] * smooth(W)
    cu, su = np.cos(th * np.outer(p, u + 1)), np.sin(th * np.outer(p, u + 1))
    rows = [sh @ c0, -(sh @ s0), -(sh @ su), -(sh @ cu)]
    cols = [sw @ c0, sw @ s0, sw @ cu, sw @ su]
    funcs, lam = [], []
    yy, xx = np.meshgrid(np.arange(P), np.arange(P), indexing="ij")
    nk = P // 2 + 1
    for kx in range(nk):
        edge = kx in (0, P // 2)
        for ky in range(P):
            if edge and ky > P // 2:
                continue
            a = 2 * np.pi * (ky * yy + kx * xx) / P
            w = np.zeros((P, nk))
            if edge:
                w[ky, kx] += 0.5
                w[(-ky) % P, kx] += 0.5
            else:
                w[ky, kx] = 1.0
            own = edge and ky in (0, P // 2)
            n = (1.0 if own else np.sqrt(2.0)) / P
            funcs.append(np.cos(a).ravel() * n)
            lam.append(w.ravel())
            if not own:
                funcs.append(np.sin(a).ravel() * n)
                lam.append(w.ravel())
    v = np.array(funcs)
    assert v.shape == (PF, PF) and np.allclose(v @ v.T, np.eye(PF))
    lam = np.array(lam).T
    v3 = v.reshape(PF, P, P)
    rr = np.stack(rows).reshape(4, H // P, P, MODES)
    cc = np.stack(cols).reshape(4, W // P, P, MODES)[:, LIVE]
    a1 = np.einsum("fyx,ksxv->ksfyv", v3, cc)
    tab = np.zeros((len(LIVE), MODES, MODES, H // P, PF))
    for k in range(4):
        for r in range(H // P):
            tab[:, :, :, r, :] += np.einsum("yu,sfyv->suvf", rr[k, r], a1[k], optimize=True)
    tab *= 0.5 / (H * W)
    tab = tab.reshape(len(LIVE), KC, KP, 2, 4 * 2 * PF).transpose(0, 3, 2, 1, 4)
    synth = tab.reshape(len(LIVE) * 2, KP, KC * 4 * 2 * PF)
    taps = np.zeros((TAPS, TAPS, 2, P, P, 2, PF))
    for dy in range(TAPS):
        for dx in range(TAPS):
            for y in range(P):
                my = y - P // 2 + dy - TAPS // 2
                role, ry = (1, my) if my >= 0 else (0, my + P)
                for x in range(P):
                    mx = x - P // 2 + dx - TAPS // 2
                    side, rx = (1, mx) if mx >= 0 else (0, mx + P)
                    taps[dy, dx, side, y, x, role] = v3[:, ry, rx]
    taps = taps.reshape(TAPS * TAPS, 2 * PF * 2 * PF)
    eight = np.zeros((1, 128))
    eight[0, 0] = eight[0, PF] = float(P)
    out = dict(basis_h=basis_h, basis_w=basis_w.reshape(W, 4 * MODES), ident=ident, flip=flip,
               sm_c=sm_c, lam=np.concatenate([lam, lam], 1), synth=synth, taps=taps, eight=eight)
    return {k: np.ascontiguousarray(a, dtype=np.float32) for k, a in out.items()}, [float(a) for a in g]


def build(nc, a, gauss, out, debug=False):
    kind = "ExternalOutput" if debug else "Internal"
    op_d = nc.dram_tensor("op_scratch", (128, C // CB, 2, CB, PF), F32, kind=kind).ap()
    coef_d = nc.dram_tensor("coef_scratch", (B, CH, 128, 128 * NX), F32, kind=kind).ap()
    z_d = nc.dram_tensor("z_scratch", (C, 128, B, NZ), F32, kind=kind).ap()
    with ExitStack() as keep:
        def sb(name, shape):
            return keep.enter_context(nc.sbuf_tensor(name, shape, F32))
        win_t = sb("win_t", [128, 2, C])
        wout_t = sb("wout_t", [128, CH, CI])
        bias_f = sb("bias_f", [128, CH, 4, 128])
        bdw = sb("bdw", [128, CH])
        bout = sb("bout", [128, 1])
        modes = sb("modes", [KP, KC, B * CI])
        operators(nc, a, op_d, win_t, wout_t, bias_f, bdw, bout)
        with nc.sbuf_tensor("pair", [CI, MODES, MODES, 2, B], F32) as pair:
            analyse(nc, a, pair)
            mix(nc, a, pair)
            smooth(nc, a, gauss, pair, modes)
        coefs(nc, a, modes, win_t, bias_f, coef_d)
        conv(nc, op_d, coef_d, z_d)
        project(nc, z_d, wout_t, bdw, bout, out)


def operators(nc, a, op_d, win_t, wout_t, bias_f, bdw, bout):
    with ExitStack() as ctx:
        def sb(name, shape):
            return ctx.enter_context(nc.sbuf_tensor(name, shape, F32))

        def sem(name):
            return ctx.enter_context(nc.semaphore(name))
        ident = sb("ident", [128, 128])
        win = sb("win", [128, CH, CI])
        wout = sb("wout", [CI, C])
        wdw = sb("wdw", [128, CH, TAPS * TAPS])
        filt = sb("filt", [128, CH, P * (P // 2 + 1)])
        lam_m = sb("lam_m", [P * (P // 2 + 1), 128])
        eight = sb("eight_sb", [1, 128])
        bin_row = sb("bin_row", [1, C])
        wdw_t = sb("wdw_t", [TAPS * TAPS, C])
        filt_t = sb("filt_t", [P * (P // 2 + 1), C])
        lam = sb("lam_sb", [128, 2, C])
        taps = sb("taps_sb", [TAPS * TAPS, PF, 128])
        ops = sb("ops", [128, C, PF])
        ps = [ctx.enter_context(nc.psum_tensor(f"op_ps{i}", [128, 2, C], F32)) for i in range(8)]
        weights_in, taps_in, trans_done, trans_kept, lam_done, lam_kept = map(
            sem, ("weights_in", "taps_in", "trans_done", "trans_kept", "lam_done", "lam_kept"))
        op_done, op_kept, op_stored = map(sem, ("op_done", "op_kept", "op_stored"))
        taps_v = a["taps"].rearrange("t (h o s) -> h t o s", h=2, s=128)
        NSMALL = 11
        block = ctx.enter_context(nc.Block())

        @block.sync
        def _(sp):
            for dst, src in (
                (ident[:], a["ident"]),
                (win[:], a["w_in"].rearrange("(h c) i -> c h i", h=CH)),
                (wout[:], a["w_out"]),
                (wdw[:], a["w_dw"].rearrange("(h c) t -> c h t", h=CH)),
                (filt[:], a["fft_filter"].rearrange("(h c) k -> c h k", h=CH)),
                (lam_m[:], a["lam"]),
                (eight[:], a["eight"]),
                (bin_row[:], a["b_in"].rearrange("(a c) -> a c", a=1)),
                (bdw[:], a["b_dw"].rearrange("(h c) -> c h", h=CH)),
                (bout[0:CI, :], a["b_out"].rearrange("(o a) -> o a", a=1)),
                (bout[CI:128, :], a["b_out"].rearrange("(o a) -> o a", a=1)),
            ):
                with nc.allow_non_contiguous_dma(reason="a few hundred words, once"):
                    sp.dma_start(dst, src).then_inc(weights_in, 16)
            for half in range(2):
                if half:
                    sp.wait_ge(op_done, 32)
                sp.dma_start(taps[:], taps_v[half]).then_inc(taps_in, 16)
                sp.wait_ge(op_kept, 32 * (half + 1))
                sp.dma_start(op_d[:, :, half].rearrange("p n c o -> p n (c o)"),
                             ops[:].rearrange("p (n c) o -> p n (c o)", c=CB)).then_inc(op_stored, 16)
                sp.wait_ge(op_stored, 16 * (half + 1))

        @block.tensor
        def _(pe):
            pe.wait_ge(weights_in, 16 * NSMALL)
            for h in range(CH):
                cs = slice(128 * h, 128 * (h + 1))
                for e in range(2):
                    nc.tensor.matmul(ps[0][e * CI:(e + 1) * CI, 0, cs], win[:, h, :], ident[:], start=True, stop=True)
                nc.tensor.matmul(ps[1][:, 0, h * CI:(h + 1) * CI], wout[:, cs], ident[0:CI, 0:CI], start=True, stop=True)
                nc.tensor.matmul(ps[2][0:TAPS * TAPS, 0, cs], wdw[:, h, :], ident[:], start=True, stop=True)
                nc.tensor.matmul(ps[3][0:P * (P // 2 + 1), 0, cs], filt[:, h, :], ident[:], start=True, stop=True)
            nc.tensor.matmul(ps[4][:, 0, :], eight[:], bin_row[:], start=True, stop=True).then_inc(trans_done, 1)
            pe.wait_ge(trans_kept, 7)
            for k in range(2):
                nc.tensor.matmul(ps[5][:, k, :], lam_m[:], filt_t[:], start=True, stop=True).then_inc(lam_done, 1)
            for half in range(2):
                pe.wait_ge(taps_in, 16 * (half + 1))
                for q in range(32):
                    n = 32 * half + q
                    if n >= 8:
                        pe.wait_ge(op_kept, n - 7)
                    elif n == 5:
                        pe.wait_ge(lam_kept, 1)
                    for k in range(2):
                        mm = nc.tensor.matmul(ps[n % 8][:, k, :], taps[:, 2 * q + k, :], wdw_t[:], start=True, stop=True)
                    mm.then_inc(op_done, 1)

        @block.vector
        def _(dve):
            dve.wait_ge(trans_done, 1)
            nc.vector.memset(win_t[:], 0.0).then_inc(trans_kept, 1)
            dve.wait_ge(trans_kept, 1)
            for dst, src in ((win_t[0:CI, 0, :], ps[0][0:CI, 0, :]),
                             (win_t[CI:128, 1, :], ps[0][CI:128, 0, :]),
                             (wout_t[:], ps[1][:, 0, 0:CH * CI].rearrange("c (h o) -> c h o", h=CH)),
                             (wdw_t[:], ps[2][0:TAPS * TAPS, 0, :]),
                             (filt_t[:], ps[3][0:P * (P // 2 + 1), 0, :])):
                nc.vector.tensor_copy(dst, src).then_inc(trans_kept, 1)
            for j in range(4):
                last = nc.vector.tensor_copy(bias_f[:, :, j, :], ps[4][:, 0, :].rearrange("p (h c) -> p h c", h=CH))
            last.then_inc(trans_kept, 1)
            dve.wait_ge(lam_done, 2)
            nc.vector.tensor_copy(lam[:], ps[5][:]).then_inc(lam_kept, 1)
            dve.wait_ge(lam_kept, 1)
            for n in range(64):
                dve.wait_ge(op_done, n + 1)
                if n == 32:
                    dve.wait_ge(op_stored, 16)
                q = n % 32
                nc.vector.tensor_tensor(ops[:, :, 2 * q:2 * q + 2].rearrange("p c k -> p k c"), ps[n % 8][:],
                                        lam[:], ALU.mult).then_inc(op_kept, 1)


def analyse(nc, a, pair):
    IT = 16
    NL = CI // IT
    F4 = 4 * MODES
    with ExitStack() as ctx:
        def sb(name, shape):
            return ctx.enter_context(nc.sbuf_tensor(name, shape, F32))

        def sem(name):
            return ctx.enter_context(nc.semaphore(name))
        xin = sb("xin", [128, NL, IT, W])
        basis_h = sb("basis_h_sb", [H, NFAST])
        basis_w = sb("basis_w_sb", [W, 4, MODES])
        flip = sb("flip_sb", [MODES, F4])
        cols = sb("cols", [W, 2, IT, 4, MODES])
        xh = sb("xh", [MODES, CI, MODES])
        col_ps = [ctx.enter_context(nc.psum_tensor(f"col_ps{i}", [W, 4, NFAST], F32)) for i in range(2)]
        xh_ps = [ctx.enter_context(nc.psum_tensor(f"xh_ps{i}", [MODES, IT, MODES], F32)) for i in range(2)]
        pair_ps = [ctx.enter_context(nc.psum_tensor(f"pair_ps{i}", [CI, MODES // 2, 2, MODES], F32)) for i in range(2)]
        basis_in = sem("basis_in")
        x_in = [sem(f"x_in{t}") for t in range(NL)]
        rows_summed = sem("rows_summed")
        cols_act, cols_dve = sem("cols_act"), sem("cols_dve")
        modes_done = sem("modes_done")
        xh_kept = sem("xh_kept")
        pair_done = sem("pair_done")
        pair_kept = sem("pair_kept")
        block = ctx.enter_context(nc.Block())

        @block.sync
        def _(sp):
            sp.dma_start(basis_h[:], a["basis_h"]).then_inc(basis_in, 16)
            sp.dma_start(basis_w[:], a["basis_w"].rearrange("w (k v) -> w k v", k=4)).then_inc(basis_in, 16)
            sp.dma_start(flip[:], a["flip"]).then_inc(basis_in, 16)
            for b in range(B):
                for t in range(NL):
                    sp.wait_ge(rows_summed, b * 16 + 4 * t + 4)
                    sp.dma_start(xin[:, t], a["x"][b, t * IT:(t + 1) * IT].rearrange("i h w -> h i w")).then_inc(x_in[t], 16)

        @block.tensor
        def _(pe):
            pe.sem_inc(rows_summed, 16)
            pe.sem_inc(modes_done, 2)
            pe.sem_inc(pair_done, 2)
            pe.wait_ge(basis_in, 48)

            def sum_rows(b, t):
                pe.wait_ge(x_in[t], b * 16 + 16)
                for g in range(4):
                    pe.wait_ge((cols_act, cols_dve)[g % 2], b * 8 + 2 * t + g // 2 + 1)
                    for k in range(4):
                        mm = nc.tensor.matmul(col_ps[g % 2][:, k, :], xin[:, t, 4 * g + k, :], basis_h[:], start=True, stop=True)
                    mm.then_inc(rows_summed, 1)

            def sum_cols(b, t):
                for s in (cols_act, cols_dve):
                    pe.wait_ge(s, b * 8 + 2 * t + 3)
                pe.wait_ge(xh_kept, b * 4 + t + 1)
                for k in range(4):
                    mm = nc.tensor.matmul(xh_ps[t % 2][:], basis_w[:, k, :], cols[:, t % 2, :, k, :], start=k == 0, stop=k == 3)
                mm.then_inc(modes_done, 1)

            with pe.Fori(0, B) as b:
                sum_rows(b, 0)
                for t in range(1, NL):
                    sum_rows(b, t)
                    sum_cols(b, t - 1)
                sum_cols(b, NL - 1)
                pe.wait_ge(xh_kept, b * 4 + 6)
                for h in range(2):
                    pe.wait_ge(pair_kept, b * 2 + h + 1)
                    for ul in range(MODES // 2):
                        u = h * (MODES // 2) + ul
                        nc.tensor.matmul(pair_ps[h][:, ul], xh[:, :, u], flip[:, 0:2 * MODES], start=True, stop=False)
                        mm = nc.tensor.matmul(pair_ps[h][:, ul], xh[:, :, (-u) % MODES], flip[:, 2 * MODES:4 * MODES],
                                              start=False, stop=True)
                    mm.then_inc(pair_done, 1)

        @block.scalar
        def _(act):
            act.sem_inc(cols_act, 1)
            act.sem_inc(pair_kept, 2)
            with act.Fori(0, B) as b:
                for t in range(NL):
                    act.wait_ge(modes_done, b * 4 + t + 1)
                    for g in (0, 2):
                        act.wait_ge(rows_summed, b * 16 + 4 * t + g + 17)
                        nc.scalar.copy(cols[:, t % 2, 4 * g:4 * g + 4].rearrange("w i k u -> w i (k u)"), col_ps[0][:, :, 0:F4])\
                          .then_inc(cols_act, 1)
                for h in range(2):
                    act.wait_ge(pair_done, b * 2 + h + 3)
                    src = pair_ps[h]
                    for ty in range(2):
                        dst = pair[:, h * (MODES // 2):(h + 1) * (MODES // 2), :, ty, bass.ds(b, 1)]
                        last = nc.scalar.copy(dst.rearrange("i u v b -> i u (v b)"), src[:, :, ty, :])
                    last.then_inc(pair_kept, 1)

        @block.vector
        def _(dve):
            dve.sem_inc(cols_dve, 1)
            dve.sem_inc(xh_kept, 2)
            with dve.Fori(0, B) as b:
                for t in range(NL):
                    dve.wait_ge(modes_done, b * 4 + t + 1)
                    for g in (1, 3):
                        dve.wait_ge(rows_summed, b * 16 + 4 * t + g + 17)
                        nc.vector.tensor_copy(cols[:, t % 2, 4 * g:4 * g + 4].rearrange("w i k u -> w i (k u)"), col_ps[1][:, :, 0:F4])\
                          .then_inc(cols_dve, 1)
                    if t > 0:
                        keep_modes(nc, dve, b, t - 1, modes_done, pair_done, xh_kept, xh, xh_ps)
                keep_modes(nc, dve, b, NL - 1, modes_done, pair_done, xh_kept, xh, xh_ps)


def keep_modes(nc, dve, b, t, modes_done, pair_done, xh_kept, xh, xh_ps):
    dve.wait_ge(modes_done, b * 4 + t + 3)
    if t == 0:
        dve.wait_ge(pair_done, b * 2 + 2)
    nc.vector.tensor_copy(xh[:, 16 * t:16 * t + 16, :], xh_ps[t % 2][:]).then_inc(xh_kept, 1)


def mix(nc, a, pair):
    with ExitStack() as ctx:
        def sb(name, shape):
            return ctx.enter_context(nc.sbuf_tensor(name, shape, F32))

        def sem(name):
            return ctx.enter_context(nc.semaphore(name))
        w1 = sb("w1", [CI, CI, MODES + 1, MODES])
        w_at = sb("w_at", [CI, 2, MODES, CI])
        sums = sb("sums", [CI, 2, MODES, 2, B])
        w_neg = sb("w_neg", [CI, 2, MODES, CI])
        mix_ps = [ctx.enter_context(nc.psum_tensor(f"mix_ps{i}", [CI, MODES, B], F32)) for i in range(2)]
        w1_in, row0, at_ready, neg_ready = map(sem, ("w1_in", "row0", "at_ready", "neg_ready"))
        sums_ready, mix_begun = sem("sums_ready"), sem("mix_begun")
        mix_done = sem("mix_done")
        mix_kept = sem("mix_kept")
        block = ctx.enter_context(nc.Block())

        @block.sync
        def _(sp):
            sp.dma_start(w1[:, :, 0:MODES, :], a["w1"]).then_inc(w1_in, 16)

        @block.gpsimd
        def _(pool):
            with pool.Fori(0, MODES // 2) as h:
                for k in range(2):
                    pool.wait_ge(mix_done, 2 * h + k + 1)
                    nc.gpsimd.tensor_copy(sums[:, k], pair[:, bass.ds(2 * h + k, 1)].rearrange("i a v k b -> i (a v) k b"))\
                      .then_inc(sums_ready, 1)

        @block.scalar
        def _(act):
            act.wait_ge(w1_in, 16)
            nc.scalar.copy(w1[:, :, MODES, :], w1[:, :, 0, :]).then_inc(row0, 1)
            act.wait_ge(row0, 1)
            with act.Fori(0, MODES // 2) as h:
                for k in range(2):
                    act.wait_ge(mix_done, 2 * h + k + 1)
                    nc.scalar.copy(w_neg[:, k].rearrange("i v o -> i o v"),
                                   w1[:, :, bass.ds(MODES - 2 * h - k, 1), :].rearrange("i o a v -> i o (a v)")).then_inc(neg_ready, 1)

        @block.tensor
        def _(pe):
            pe.sem_inc(mix_done, 2)
            with pe.Fori(0, MODES // 2) as h:
                for k in range(2):
                    pe.wait_ge(at_ready, 2 * h + k + 1)
                    pe.wait_ge(neg_ready, 2 * h + k + 1)
                    pe.wait_ge(sums_ready, 2 * h + k + 1)
                    pe.wait_ge(mix_kept, 2 * h + k + 1)
                    pe.sem_inc(mix_begun, 1)
                    for v in range(MODES):
                        dst = mix_ps[k][:, v, :]
                        nc.tensor.matmul(dst, w_at[:, k, v, :], sums[:, k, v, 0, :], start=True, stop=False)
                        mm = nc.tensor.matmul(dst, w_neg[:, k, (-v) % MODES, :], sums[:, k, v, 1, :], start=False, stop=True)
                    mm.then_inc(mix_done, 1)

        @block.vector
        def _(dve):
            dve.sem_inc(mix_kept, 2)
            dve.wait_ge(w1_in, 16)
            with dve.Fori(0, MODES // 2) as h:
                for k in range(2):
                    dve.wait_ge(mix_done, 2 * h + k + 1)
                    nc.vector.tensor_copy(w_at[:, k].rearrange("i v o -> i o v"),
                                          w1[:, :, bass.ds(2 * h + k, 1), :].rearrange("i o a v -> i o (a v)")).then_inc(at_ready, 1)
                    dve.wait_ge(mix_done, 2 * h + k + 3)
                    nc.vector.tensor_copy(pair[:, bass.ds(2 * h + k, 1), :, 0, :].rearrange("o a v b -> o (a v) b"),
                                          mix_ps[k][:]).then_inc(mix_kept, 1)


def smooth(nc, a, gauss, pair, modes):
    with ExitStack() as ctx:
        def sb(name, shape):
            return ctx.enter_context(nc.sbuf_tensor(name, shape, F32))

        def sem(name):
            return ctx.enter_context(nc.semaphore(name))
        sm_c = sb("sm_c_sb", [CI, CI])
        padded = sb("padded", [KP, KC, B + 2 * R, CI])
        ps = [ctx.enter_context(nc.psum_tensor(f"chan_ps{i}", [128, 8, CI], F32)) for i in range(8)]
        smc_in, chan_done, chan_kept, step = map(sem, ("smc_in", "chan_done", "chan_kept", "smooth_step"))
        mixed = pair[:].rearrange("o u v k b -> o (u v) k b")
        block = ctx.enter_context(nc.Block())

        @block.sync
        def _(sp):
            sp.dma_start(sm_c[:], a["sm_c"]).then_inc(smc_in, 16)

        @block.tensor
        def _(pe):
            pe.wait_ge(smc_in, 16)
            for n in range(8):
                for b in range(8):
                    mm = nc.tensor.matmul(ps[n][0:KP, b, :], mixed[:, (n // 2) * KP:(n // 2 + 1) * KP, 0, 8 * (n % 2) + b],
                                          sm_c[:], start=True, stop=True)
                mm.then_inc(chan_done, 1)

        @block.vector
        def _(dve):
            for n in range(8):
                dve.wait_ge(chan_done, n + 1)
                b0 = R + 8 * (n % 2)
                nc.vector.tensor_copy(padded[:, n // 2, b0:b0 + 8, :], ps[n][0:KP]).then_inc(chan_kept, 1)
            dve.wait_ge(chan_kept, 8)
            for b in range(R):
                nc.vector.tensor_copy(padded[:, :, b, :], padded[:, :, R, :]).then_inc(chan_kept, 1)
                nc.vector.tensor_copy(padded[:, :, B + R + b, :], padded[:, :, B + R - 1, :]).then_inc(chan_kept, 1)
            dve.wait_ge(chan_kept, 8 + 2 * R)

            def at(t):
                return padded[:, :, t:t + B, :].rearrange("m k b o -> m k (b o)")
            nc.vector.tensor_scalar(modes[:], at(0), gauss[0], None, ALU.mult).then_inc(step, 1)
            for t in range(1, 2 * R + 1):
                dve.wait_ge(step, t)
                nc.vector.scalar_tensor_tensor(modes[:], at(t), gauss[t], modes[:], ALU.mult, ALU.add).then_inc(step, 1)


def coefs(nc, a, modes, win_t, bias_f, coef_d):
    NCH = 2 * len(LIVE)
    PIECE = 4 * 2 * PF
    with ExitStack() as ctx:
        def sb(name, shape):
            return ctx.enter_context(nc.sbuf_tensor(name, shape, F32))

        def sem(name):
            return ctx.enter_context(nc.semaphore(name))
        synth = sb("synth_sb", [KP, 2, KC, PIECE])
        now = sb("now", [KP, KC, 128])
        y = sb("y", [128, NCH, PIECE])
        st = [sb(f"coef_st{h}", [128, 128, NS, NJ]) for h in range(CH)]
        y_ps = [ctx.enter_context(nc.psum_tensor(f"y_ps{i}", [128, PIECE], F32)) for i in range(4)]
        c_ps = [ctx.enter_context(nc.psum_tensor(f"c_ps{i}", [128, 4, 128], F32)) for i in range(4)]
        synth_in = [sem(f"synth_in{i}") for i in range(2)]
        stored = sem("coef_stored")
        st_free = [sem(f"st_free{i}") for i in range(CH)]
        now_ready = sem("now_ready")
        y_done = sem("y_done")
        y_kept = sem("y_kept")
        c_done = sem("c_done")
        c_kept = sem("c_kept")
        const_set = sem("const_set")
        block = ctx.enter_context(nc.Block())

        @block.sync
        def _(sp):
            with sp.Fori(0, B // 2) as i:
                for n in range(NCH):
                    sp.wait_ge(y_done, i * NCH + n + NCH - 1)
                    sp.dma_start(synth[:, n % 2], a["synth"][n].rearrange("m (k p) -> m k p", k=KC)).then_inc(synth_in[n % 2], 16)

        @block.gpsimd
        def _(pool):
            with pool.Fori(0, B // 2) as i:
                for e in range(2):
                    for h in range(CH):
                        pool.wait_ge(c_kept, i * 4 * NCH + (2 * e + h + 1) * NCH + 4)
                        pool.dma_start(coef_d[bass.ds(2 * i + e, 1), h].rearrange("b p n -> p (b n)"),
                                       st[h][:].rearrange("p c s j -> p (c s j)")).then_inc(stored, 16)
                        pool.wait_ge(stored, i * 64 + (2 * e + h + 1) * 16)
                        pool.sem_inc(st_free[h], 1)

        @block.tensor
        def _(pe):
            pe.sem_inc(y_done, NCH)
            pe.sem_inc(c_done, 4 * NCH)
            with pe.Fori(0, B // 2) as i:
                pe.wait_ge(now_ready, i + 1)
                for n in range(NCH):
                    pe.wait_ge(synth_in[n % 2], i * 16 * (NCH // 2) + 16 * (n // 2) + 16)
                    pe.wait_ge(y_kept, i * NCH + n + 1)
                    for k in range(KC):
                        mm = nc.tensor.matmul(y_ps[n % 4][:], now[:, k, :], synth[:, n % 2, k, :], start=k == 0, stop=k == KC - 1)
                    mm.then_inc(y_done, 1)
                pe.wait_ge(y_kept, (i + 1) * NCH + 4)
                for e in range(2):
                    for h in range(CH):
                        for n in range(NCH):
                            q = (2 * e + h) * NCH + n
                            pe.wait_ge(c_kept, i * 4 * NCH + q + 1)
                            for j in range(4):
                                mm = nc.tensor.matmul(c_ps[q % 4][:, j, :], y[:, n, j * 128:(j + 1) * 128],
                                                      win_t[:, e, h * 128:(h + 1) * 128], start=True, stop=True)
                            mm.then_inc(c_done, 1)

        @block.scalar
        def _(act):
            act.sem_inc(y_kept, 4)
            with act.Fori(0, B // 2) as i:
                act.wait_ge(y_done, i * NCH + NCH)
                nc.scalar.copy(now[:], modes[:, :, bass.ds(i * 128, 128)]).then_inc(now_ready, 1)
                act.wait_ge(c_done, (i + 1) * 4 * NCH)
                for n in range(NCH):
                    act.wait_ge(y_done, i * NCH + n + 1 + NCH)
                    nc.scalar.copy(y[:, n, :], y_ps[n % 4][:]).then_inc(y_kept, 1)

        @block.vector
        def _(dve):
            dve.sem_inc(c_kept, 4)
            for h in range(CH):
                dve.sem_inc(st_free[h], 1)
            for h in range(CH):
                for s in range(CONST0, CONST0 + NCONST):
                    for j in range(0, NJ, 4):
                        nc.vector.tensor_copy(st[h][:, :, s, j:j + 4].rearrange("p c j -> p j c"), bias_f[:, h])\
                          .then_inc(const_set, 1)
            with dve.Fori(0, B // 2) as i:
                for e in range(2):
                    for h in range(CH):
                        dve.wait_ge(st_free[h], 2 * i + e + 1)
                        for n in range(NCH):
                            q = (2 * e + h) * NCH + n
                            dve.wait_ge(c_done, i * 4 * NCH + q + 1 + 4 * NCH)
                            j = 4 * (n % 2)
                            nc.vector.tensor_tensor(st[h][:, :, SLOT[n // 2], j:j + 4].rearrange("p c j -> p j c"),
                                                    c_ps[q % 4][:], bias_f[:, h], ALU.add).then_inc(c_kept, 1)


def conv(nc, op_d, coef_d, z_d):
    NCB = C // CB
    BG = 4
    NG = B // BG
    PER = CB * NG
    ZR = 4
    LAST = NCB // 2 - 1
    with ExitStack() as ctx:
        def sb(name, shape):
            return ctx.enter_context(nc.sbuf_tensor(name, shape, F32))

        def sem(name):
            return ctx.enter_context(nc.semaphore(name))
        xs = [sb(f"xs{i}", [128, B, CB, NX]) for i in range(2)]
        xsh = [sb(f"xsh{i}", [128, B, CB, NS, NJ + 1]) for i in range(2)]
        op = [sb(f"op{i}", [128, 2, CB, PF]) for i in range(2)]
        z = sb("z_st", [128, ZR, B, NT, NJ])
        z_top = sb("z_top", [32, ZR, B, NT, NJ])
        ps = [ctx.enter_context(nc.psum_tensor(f"z_ps{i}", [128, 512], F32)) for i in range(8)]
        xs_in = [sem(f"xs_in{i}") for i in range(2)]
        op_in = [sem(f"op_in{i}") for i in range(2)]
        stored = [sem(f"z_stored{i}") for i in range(ZR)]
        z_done = sem("z_done")
        z_act, z_dve = sem("z_act"), sem("z_dve")
        up_done, down_done = sem("up_done"), sem("down_done")
        zero_set = sem("zero_set")
        block = ctx.enter_context(nc.Block())

        @block.sync
        def _(sp):
            for r in range(ZR):
                sp.sem_inc(stored[r], 32)

            def load(i, k):
                sp.wait_ge(z_done, i * (2 * PER) + (k + 1) * PER)
                sp.dma_start(xs[k][:].rearrange("p b c n -> p b (c n)"),
                             coef_d[:, k, :, bass.ds(i * (CB * NX), CB * NX)].rearrange("b p n -> p b n"))\
                  .then_inc(xs_in[k], 16)
                sp.dma_start(op[k][:].rearrange("p s c o -> p (s c o)"),
                             op_d[:, bass.ds(i + k * (NCB // 2), 1)].rearrange("p n s c o -> p (n s c o)")).then_inc(op_in[k], 16)

            def store(i, k):
                for c in range(CB):
                    r = c % ZR
                    for kept in (z_act, z_dve):
                        sp.wait_ge(kept, i * (2 * CB * 4) + 4 * (k * CB + c) + 12)
                    dst = z_d[bass.ds(i * CB + k * 128 + c, 1)].rearrange("c p b n -> (c p) b n")
                    sp.dma_start(dst[0:32], z_top[:, r].rearrange("p b t j -> p b (t j)")).then_inc(stored[r], 16)
                    sp.dma_start(dst[32:128], z[32:128, r].rearrange("p b t j -> p b (t j)")).then_inc(stored[r], 16)

            load(0, 0)
            load(0, 1)
            with sp.Fori(0, LAST) as i:
                store(i, 0)
                load(i + 1, 0)
                store(i, 1)
                load(i + 1, 1)
            store(LAST, 0)
            store(LAST, 1)
            for r in range(ZR):
                sp.wait_ge(stored[r], 32 * (C // ZR) + 32)

        @block.tensor
        def _(pe):
            pe.sem_inc(z_done, 2 * PER)
            with pe.Fori(0, NCB // 2) as i:
                for k in range(2):
                    pe.wait_ge(op_in[k], i * 16 + 16)
                    pe.wait_ge(xs_in[k], i * 16 + 16)
                    for c in range(CB):
                        cl = k * CB + c
                        pe.wait_ge(up_done, i * (2 * CB) + cl + 1)
                        pe.wait_ge(down_done, i * (2 * CB) + cl + 1)
                        for g in range(NG):
                            pe.wait_ge((z_act, z_dve)[g % 2], i * (2 * CB * 4) + 4 * cl + 2 * (g // 2) + 2)
                            tile = ps[(cl * NG + g) % 8][:, 0:BG * NT * (NJ + 1)].rearrange("p (b t j) -> p b t j", b=BG, t=NT)
                            bs = slice(g * BG, (g + 1) * BG)
                            nat = xs[k][:, bs, c, :].rearrange("p b (s j) -> p b s j", s=NS)
                            for side, ts in ((0, slice(1, NT)), (1, slice(0, NS))):
                                nc.tensor.matmul(tile[0:PF, :, ts, :], op[k][:, side, c, :], xsh[k][:, bs, c],
                                                 start=side == 0, stop=side == 1, skip_group_check=True)
                                mm = nc.tensor.matmul(tile[PF:128, :, ts, 0:NJ], op[k][:, side, c, :], nat,
                                                      start=side == 0, stop=side == 1, skip_group_check=True)
                            mm.then_inc(z_done, 1)

        def shift(copy, eng, i, k, c, done, up):
            if c == 0:
                eng.wait_ge(xs_in[k], i * 16 + 16)
            nat = xs[k][:, :, c, :].rearrange("p b (s j) -> p b s j", s=NS)
            if up:
                copy(xsh[k][0:PF, :, c, :, 1:NJ + 1], nat[PF:128]).then_inc(done, 1)
            else:
                copy(xsh[k][PF:128, :, c, :, 0:NJ], nat[0:PF]).then_inc(done, 1)

        def evacuate(copy, eng, kept, done, up):
            def of_load(i, k, following):
                for c in range(CB):
                    cl = k * CB + c
                    r = cl % ZR
                    eng.wait_ge(stored[r], i * (2 * CB // ZR * 32) + 32 * (cl // ZR) + 32)
                    for g in ((0, 2) if up else (1, 3)):
                        tile = ps[(cl * NG + g) % 8][:, 0:BG * NT * (NJ + 1)].rearrange("p (b t j) -> p b t j", b=BG, t=NT)
                        bs = slice(g * BG, (g + 1) * BG)
                        eng.wait_ge(z_done, i * (2 * PER) + cl * NG + g + 1 + 2 * PER)
                        copy(z[:, r, bs], tile[:, :, :, 0:NJ]).then_inc(kept, 1)
                        copy(z_top[:, r, bs], tile[0:32, :, :, 1:NJ + 1]).then_inc(kept, 1)
                    if following:
                        shift(copy, eng, *following, c, done, up)

            for c in range(CB):
                shift(copy, eng, 0, 0, c, done, up)
            with eng.Fori(0, LAST) as i:
                of_load(i, 0, (i, 1))
                of_load(i, 1, (i + 1, 0))
            of_load(LAST, 0, (LAST, 1))
            of_load(LAST, 1, None)

        @block.scalar
        def _(act):
            act.sem_inc(z_act, 8)
            act.wait_ge(zero_set, 4)
            evacuate(nc.scalar.copy, act, z_act, up_done, True)

        @block.vector
        def _(dve):
            dve.sem_inc(z_dve, 8)
            for k in range(2):
                nc.vector.memset(xsh[k][0:PF, :, :, :, 0], 0.0).then_inc(zero_set, 1)
                nc.vector.memset(xsh[k][PF:128, :, :, :, NJ], 0.0).then_inc(zero_set, 1)
            dve.wait_ge(zero_set, 4)
            evacuate(nc.vector.tensor_copy, dve, z_dve, down_done, False)


def project(nc, z_d, wout_t, bdw, bout, out):
    PX = 8
    NL = 2 * P
    ZB = 4
    with ExitStack() as ctx:
        def sb(name, shape):
            return ctx.enter_context(nc.sbuf_tensor(name, shape, F32))

        def sem(name):
            return ctx.enter_context(nc.semaphore(name))
        zt = [sb(f"zt{i}", [128, CH, PX, 2, NZ]) for i in range(ZB)]
        img = [sb(f"img{i}", [128, H, W]) for i in range(2)]
        ps = [ctx.enter_context(nc.psum_tensor(f"o_ps{i}", [128, 512], F32)) for i in range(8)]
        z_in = [sem(f"z_in{i}") for i in range(ZB)]
        stored = sem("img_stored")
        img_free = [sem(f"img_free{i}") for i in range(2)]
        act_done = sem("gelu_done")
        o_done = sem("o_done")
        o_kept = sem("o_kept")
        block = ctx.enter_context(nc.Block())
        z_v = z_d.rearrange("(h c) x b n -> c h x b n", h=CH)

        @block.sync
        def _(sp):
            with sp.Fori(0, B // 4) as i:
                for k in range(2):
                    for n in range(NL):
                        m = k * NL + n
                        sp.wait_ge(o_done, i * (4 * NL) + 2 * m + 2)
                        for h in range(CH):
                            src = z_v[:, h, n * PX:(n + 1) * PX, bass.ds(4 * i + 2 * k, 2)]
                            sp.dma_start(zt[m % ZB][:, h], src).then_inc(z_in[m % ZB], 16)

        @block.gpsimd
        def _(pool):
            with pool.Fori(0, B // 4) as i:
                for k in range(2):
                    pool.wait_ge(o_kept, i * (4 * NL) + (k + 1) * 2 * NL + 8)
                    pool.dma_start(out[bass.ds(4 * i + 2 * k, 2)].rearrange("b o h w -> (b o) (h w)"),
                                   img[k][:].rearrange("p h w -> p (h w)")).then_inc(stored, 16)
                    pool.wait_ge(stored, i * 32 + 16 * (k + 1))
                    pool.sem_inc(img_free[k], 1)

        @block.scalar
        def _(act):
            with act.Fori(0, B // 4) as i:
                for m in range(2 * NL):
                    act.wait_ge(z_in[m % ZB], i * (2 * NL // ZB * 32) + 32 * (m // ZB) + 32)
                    for h in range(CH):
                        v = zt[m % ZB][:, h].rearrange("c x b n -> c (x b n)")
                        nc.scalar.activation(v, v, ACT.Gelu, bias=bdw[:, h:h + 1]).then_inc(act_done, 1)

        @block.tensor
        def _(pe):
            pe.sem_inc(o_done, 2 * ZB)
            with pe.Fori(0, B // 4) as i:
                for m in range(2 * NL):
                    pe.wait_ge(act_done, i * (4 * NL) + 2 * m + 2)
                    for q in range(2):
                        n = 2 * m + q
                        pe.wait_ge(o_kept, i * (4 * NL) + n + 1)
                        for h in range(CH):
                            for e in range(2):
                                mm = nc.tensor.matmul(ps[n % 8][e * CI:(e + 1) * CI, 0:4 * NZ].rearrange("o (x n) -> o x n", x=4),
                                                      wout_t[:, h, :], zt[m % ZB][:, h, 4 * q:4 * q + 4, e, :],
                                                      start=h == 0, stop=h == CH - 1)
                        mm.then_inc(o_done, 1)

        @block.vector
        def _(dve):
            dve.sem_inc(o_kept, 8)
            for k in range(2):
                dve.sem_inc(img_free[k], 1)
            with dve.Fori(0, B // 4) as i:
                for k in range(2):
                    dve.wait_ge(img_free[k], i + 1)
                    for n in range(NL):
                        first = n - P // 2 if n >= P // 2 else n - P // 2 + 2 * P
                        rows = img[k][:, first::2 * P, :]
                        groups = rows.rearrange("p j (g x) -> p x g j", x=4)
                        for q in range(2):
                            m = 2 * (k * NL + n) + q
                            dve.wait_ge(o_done, i * (4 * NL) + m + 1 + 2 * ZB)
                            src = ps[m % 8][:, 0:4 * NZ].rearrange("p (x t j) -> p x t j", x=4, t=NT)
                            if q == 0:
                                pieces = ((slice(1, 6), groups[:, :, 1:11:2, :]), (slice(7, 12), groups[:, :, 23:32:2, :]))
                            else:
                                pieces = ((slice(0, 6), groups[:, :, 0:12:2, :]), (slice(7, 11), groups[:, :, 24:32:2, :]))
                            for ts, dst in pieces:
                                last = nc.vector.tensor_scalar(dst, src[:, :, ts, :], bout[:, 0:1], None, ALU.add)
                                if q == 0 and ts.start == 1:
                                    mid = src[:, 0, 6, :].unsqueeze(2).broadcast_to([128, NJ, MID1 - MID0])
                                    nc.vector.tensor_scalar(rows[:, :, MID0:MID1], mid, bout[:, 0:1], None, ALU.add)
                            last.then_inc(o_kept, 1)


NAMES = {"x": "x", "w1": "L0_conv_w1", "w_in": "L1_conv_w_in", "b_in": "L1_conv_b_in",
         "fft_filter": "L1_conv_fft_filter", "w_dw": "L1_conv_w_dw", "b_dw": "L1_conv_b_dw",
         "w_out": "L1_conv_w_out", "b_out": "L1_conv_b_out"}
DEBUG = False


def kernel(**inputs):
    import numpy as np
    import concourse.bacc as bacc
    from concourse.bass_utils import run_bass_kernel_spmd

    nc = bacc.Bacc("TRN2", target_bir_lowering=False, num_devices=1)
    arrays, aps = {}, {}
    tables, gauss = constants()
    given = {k: np.ascontiguousarray(inputs[v]) for k, v in NAMES.items()}
    for k in ("w_in", "w_out"):
        given[k] = given[k].reshape(given[k].shape[:2])
    for k in ("fft_filter", "w_dw"):
        given[k] = given[k].reshape(C, -1)
    for k, v in {**given, **tables}.items():
        arrays[f"in_{k}"] = v
        aps[k] = nc.dram_tensor(f"in_{k}", v.shape, F32, kind="ExternalInput").ap()
    out = nc.dram_tensor("out", (B, CI, H, W), F32, kind="ExternalOutput").ap()
    build(nc, aps, gauss, out, DEBUG)
    r = run_bass_kernel_spmd(nc, [arrays], core_ids=[0])
    return r.results[0]["out"]
```

```python
from contextlib import ExitStack

import concourse.bass as bass
from concourse import mybir

F32 = mybir.dt.float32
ACT = mybir.ActivationFunctionType
ALU = mybir.AluOpType

B, CI, H, W = 16, 64, 128, 128
C = 256
CH = C // 128
MODES = 20
NM = MODES * MODES
KC, KP = 4, NM // 4
P = 8
PF = P * P
NJ = H // (2 * P)
R = 4
TAPS = 7
LIVE = [0, 1, 2, 3, 4, 12, 13, 14, 15]
SLOT = [0, 1, 2, 3, 4, 7, 8, 9, 10]
CONST0, NCONST = 5, 2
NS = len(LIVE) + NCONST
NT = NS + 1
NX = NS * NJ
NZ = NT * NJ
CB = 4
NFAST = 96
MID0, MID1 = 44, 92


def constants():
    import numpy as np
    th = 2 * np.pi / W
    t = np.arange(-R, R + 1, dtype=np.float32)
    g = np.exp(-0.5 * t ** 2)
    g = (g / g.sum()).astype(np.float64)

    def smooth(n):
        m = np.zeros((n, n))
        for i in range(n):
            for k in range(2 * R + 1):
                m[i, min(max(i + k - R, 0), n - 1)] += g[k]
        return m

    u = np.arange(MODES)
    p = np.arange(H)
    c0, s0 = np.cos(th * np.outer(p, u)), np.sin(th * np.outer(p, u))
    c1, s1 = np.cos(th * np.outer(p + 1, u)), np.sin(th * np.outer(p + 1, u))
    basis_h = np.concatenate([c0, s0, c1, s1, np.zeros((H, NFAST - 4 * MODES))], 1)
    basis_w = np.stack([c0, -s0, -s1, -c1], 1)
    ident = np.eye(128)
    sm_c = np.concatenate([smooth(CI).T, np.zeros((CI, NFAST - CI))], 1)
    sh = smooth(H)
    mask = (np.abs(np.fft.fftfreq(W)) <= 0.25).astype(np.float64)
    sw = mask[:, None] * smooth(W)
    cu, su = np.cos(th * np.outer(p, u + 1)), np.sin(th * np.outer(p, u + 1))
    rows = [sh @ c0, -(sh @ s0), -(sh @ su), -(sh @ cu)]
    cols = [sw @ c0, sw @ s0, sw @ cu, sw @ su]
    funcs, lam = [], []
    yy, xx = np.meshgrid(np.arange(P), np.arange(P), indexing="ij")
    nk = P // 2 + 1
    for kx in range(nk):
        edge = kx in (0, P // 2)
        for ky in range(P):
            if edge and ky > P // 2:
                continue
            a = 2 * np.pi * (ky * yy + kx * xx) / P
            w = np.zeros((P, nk))
            if edge:
                w[ky, kx] += 0.5
                w[(-ky) % P, kx] += 0.5
            else:
                w[ky, kx] = 1.0
            own = edge and ky in (0, P // 2)
            n = (1.0 if own else np.sqrt(2.0)) / P
            funcs.append(np.cos(a).ravel() * n)
            lam.append(w.ravel())
            if not own:
                funcs.append(np.sin(a).ravel() * n)
                lam.append(w.ravel())
    v = np.array(funcs)
    assert v.shape == (PF, PF) and np.allclose(v @ v.T, np.eye(PF))
    lam = np.array(lam).T
    v3 = v.reshape(PF, P, P)
    rr = np.stack(rows).reshape(4, H // P, P, MODES)
    cc = np.stack(cols).reshape(4, W // P, P, MODES)[:, LIVE]
    a1 = np.einsum("fyx,ksxv->ksfyv", v3, cc)
    tab = np.zeros((len(LIVE), MODES, MODES, H // P, PF))
    for k in range(4):
        for r in range(H // P):
            tab[:, :, :, r, :] += np.einsum("yu,sfyv->suvf", rr[k, r], a1[k], optimize=True)
    tab *= 0.5 / (H * W)
    tab = tab.reshape(len(LIVE), KC, KP, 2, 4 * 2 * PF).transpose(0, 3, 2, 1, 4)
    synth = tab.reshape(len(LIVE) * 2, KP, KC * 4 * 2 * PF)
    taps = np.zeros((TAPS, TAPS, 2, P, P, 2, PF))
    for dy in range(TAPS):
        for dx in range(TAPS):
            for y in range(P):
                my = y - P // 2 + dy - TAPS // 2
                role, ry = (1, my) if my >= 0 else (0, my + P)
                for x in range(P):
                    mx = x - P // 2 + dx - TAPS // 2
                    side, rx = (1, mx) if mx >= 0 else (0, mx + P)
                    taps[dy, dx, side, y, x, role] = v3[:, ry, rx]
    taps = taps.reshape(TAPS * TAPS, 2 * PF * 2 * PF)
    eight = np.zeros((1, 128))
    eight[0, 0] = eight[0, PF] = float(P)
    out = dict(basis_h=basis_h, basis_w=basis_w.reshape(W, 4 * MODES), ident=ident,
               sm_c=sm_c, lam=np.concatenate([lam, lam], 1), synth=synth, taps=taps, eight=eight)
    return {k: np.ascontiguousarray(a, dtype=np.float32) for k, a in out.items()}, [float(a) for a in g]


def build(nc, a, gauss, out, debug=False):
    kind = "ExternalOutput" if debug else "Internal"
    op_d = nc.dram_tensor("op_scratch", (128, C // CB, 2, CB, PF), F32, kind=kind).ap()
    coef_d = nc.dram_tensor("coef_scratch", (B, CH, 128, 128 * NX), F32, kind=kind).ap()
    z_d = nc.dram_tensor("z_scratch", (C, 128, B, NZ), F32, kind=kind).ap()
    with ExitStack() as keep:
        def sb(name, shape):
            return keep.enter_context(nc.sbuf_tensor(name, shape, F32))
        win_t = sb("win_t", [128, 2, C])
        wout_t = sb("wout_t", [128, CH, CI])
        bias_f = sb("bias_f", [128, CH, 4, 128])
        bdw = sb("bdw", [128, CH])
        bout = sb("bout", [128, 1])
        modes = sb("modes", [KP, KC, B * CI])
        operators(nc, a, op_d, win_t, wout_t, bias_f, bdw, bout)
        with nc.sbuf_tensor("pair", [CI, MODES, MODES, 2, B], F32) as pair:
            with nc.sbuf_tensor("w1", [CI, CI, NM], F32) as w1:
                analyse(nc, a, pair, w1)
                mix(nc, pair, w1)
            smooth(nc, a, gauss, pair, modes)
        coefs(nc, a, modes, win_t, bias_f, coef_d)
        conv(nc, op_d, coef_d, z_d)
        project(nc, z_d, wout_t, bdw, bout, out)


def operators(nc, a, op_d, win_t, wout_t, bias_f, bdw, bout):
    with ExitStack() as ctx:
        def sb(name, shape):
            return ctx.enter_context(nc.sbuf_tensor(name, shape, F32))

        def sem(name):
            return ctx.enter_context(nc.semaphore(name))
        ident = sb("ident", [128, 128])
        win = sb("win", [128, CH, CI])
        wout = sb("wout", [CI, C])
        wdw = sb("wdw", [128, CH, TAPS * TAPS])
        filt = sb("filt", [128, CH, P * (P // 2 + 1)])
        lam_m = sb("lam_m", [P * (P // 2 + 1), 128])
        eight = sb("eight_sb", [1, 128])
        bin_row = sb("bin_row", [1, C])
        wdw_t = sb("wdw_t", [TAPS * TAPS, C])
        filt_t = sb("filt_t", [P * (P // 2 + 1), C])
        lam = sb("lam_sb", [128, 2, C])
        taps = sb("taps_sb", [TAPS * TAPS, 2, PF // 2, 128])
        ops = [sb(f"ops{side}", [128, C, PF]) for side in range(2)]
        ps = [ctx.enter_context(nc.psum_tensor(f"op_ps{i}", [128, 2, C], F32)) for i in range(8)]
        weights_in, taps_in0, trans_done, trans_kept, lam_done, lam_kept = map(
            sem, ("weights_in", "taps_in0", "trans_done", "trans_kept", "lam_done", "lam_kept"))
        op_done, op_kept, op_stored = map(sem, ("op_done", "op_kept", "op_stored"))
        taps_v = a["taps"].rearrange("t (q o s) -> q t o s", q=4, s=128)
        NSMALL = 11
        taps_in = (taps_in0, sem("taps_in1"))
        block = ctx.enter_context(nc.Block())

        @block.sync
        def _(sp):
            for dst, src in (
                (ident[:], a["ident"]),
                (win[:], a["w_in"].rearrange("(h c) i -> c h i", h=CH)),
                (wout[:], a["w_out"]),
                (wdw[:], a["w_dw"].rearrange("(h c) t -> c h t", h=CH)),
                (filt[:], a["fft_filter"].rearrange("(h c) k -> c h k", h=CH)),
                (lam_m[:], a["lam"]),
                (eight[:], a["eight"]),
                (bin_row[:], a["b_in"].rearrange("(a c) -> a c", a=1)),
                (bdw[:], a["b_dw"].rearrange("(h c) -> c h", h=CH)),
                (bout[0:CI, :], a["b_out"].rearrange("(o a) -> o a", a=1)),
                (bout[CI:128, :], a["b_out"].rearrange("(o a) -> o a", a=1)),
            ):
                with nc.allow_non_contiguous_dma(reason="a few hundred words, once"):
                    sp.dma_start(dst, src).then_inc(weights_in, 16)
            for side in range(2):
                sp.wait_ge(op_kept, 32 * (side + 1))
                sp.dma_start(op_d[:, :, side].rearrange("p n c o -> p n (c o)"),
                             ops[side][:].rearrange("p (n c) o -> p n (c o)", c=CB)).then_inc(op_stored, 16)
            sp.wait_ge(op_stored, 32)

        @block.gpsimd
        def _(pool):
            for q in range(4):
                if q >= 2:
                    pool.wait_ge(op_done, 16 * (q - 1))
                pool.dma_start(taps[:, q % 2], taps_v[q]).then_inc(taps_in[q % 2], 16)

        @block.tensor
        def _(pe):
            pe.wait_ge(weights_in, 16 * NSMALL)
            for h in range(CH):
                cs = slice(128 * h, 128 * (h + 1))
                for e in range(2):
                    nc.tensor.matmul(ps[0][e * CI:(e + 1) * CI, 0, cs], win[:, h, :], ident[:], start=True, stop=True)
                nc.tensor.matmul(ps[1][:, 0, h * CI:(h + 1) * CI], wout[:, cs], ident[0:CI, 0:CI], start=True, stop=True)
                nc.tensor.matmul(ps[2][0:TAPS * TAPS, 0, cs], wdw[:, h, :], ident[:], start=True, stop=True)
                nc.tensor.matmul(ps[3][0:P * (P // 2 + 1), 0, cs], filt[:, h, :], ident[:], start=True, stop=True)
            nc.tensor.matmul(ps[4][:, 0, :], eight[:], bin_row[:], start=True, stop=True).then_inc(trans_done, 1)
            pe.wait_ge(trans_kept, 7)
            for k in range(2):
                nc.tensor.matmul(ps[5][:, k, :], lam_m[:], filt_t[:], start=True, stop=True).then_inc(lam_done, 1)
            for half in range(2):
                for q in range(32):
                    n = 32 * half + q
                    if n % 16 == 0:
                        pe.wait_ge(taps_in[n // 16 % 2], 16 * (n // 32 + 1))
                    if n >= 8:
                        pe.wait_ge(op_kept, n - 7)
                    elif n == 5:
                        pe.wait_ge(lam_kept, 1)
                    for k in range(2):
                        mm = nc.tensor.matmul(ps[n % 8][:, k, :], taps[:, n // 16 % 2, 2 * (n % 16) + k, :], wdw_t[:], start=True, stop=True)
                    mm.then_inc(op_done, 1)

        @block.vector
        def _(dve):
            dve.wait_ge(trans_done, 1)
            nc.vector.memset(win_t[:], 0.0).then_inc(trans_kept, 1)
            dve.wait_ge(trans_kept, 1)
            for dst, src in ((win_t[0:CI, 0, :], ps[0][0:CI, 0, :]),
                             (win_t[CI:128, 1, :], ps[0][CI:128, 0, :]),
                             (wout_t[:], ps[1][:, 0, 0:CH * CI].rearrange("c (h o) -> c h o", h=CH)),
                             (wdw_t[:], ps[2][0:TAPS * TAPS, 0, :]),
                             (filt_t[:], ps[3][0:P * (P // 2 + 1), 0, :])):
                nc.vector.tensor_copy(dst, src).then_inc(trans_kept, 1)
            for j in range(4):
                last = nc.vector.tensor_copy(bias_f[:, :, j, :], ps[4][:, 0, :].rearrange("p (h c) -> p h c", h=CH))
            last.then_inc(trans_kept, 1)
            dve.wait_ge(lam_done, 2)
            nc.vector.tensor_copy(lam[:], ps[5][:]).then_inc(lam_kept, 1)
            dve.wait_ge(lam_kept, 1)
            for n in range(64):
                dve.wait_ge(op_done, n + 1)
                q = n % 32
                nc.vector.tensor_tensor(ops[n // 32][:, :, 2 * q:2 * q + 2].rearrange("p c k -> p k c"), ps[n % 8][:],
                                        lam[:], ALU.mult).then_inc(op_kept, 1)


def analyse(nc, a, pair, w1):
    IT = 8
    NL = CI // IT
    NX_IN = 4
    F4 = 4 * MODES
    Q = 32
    with ExitStack() as ctx:
        def sb(name, shape):
            return ctx.enter_context(nc.sbuf_tensor(name, shape, F32))

        def sem(name):
            return ctx.enter_context(nc.semaphore(name))
        xin = sb("xin", [128, NX_IN, IT, W])
        basis_h = sb("basis_h_sb", [H, NFAST])
        basis_w = sb("basis_w_sb", [W, 4, MODES])
        ident = sb("ident_m", [MODES, MODES])
        cols = sb("cols", [W, 4, IT, 4, MODES])
        xh = sb("xh", [MODES, NL, IT, MODES])
        col_ps = [ctx.enter_context(nc.psum_tensor(f"col_ps{i}", [W, 4, NFAST], F32)) for i in range(4)]
        xh_ps = [ctx.enter_context(nc.psum_tensor(f"xh_ps{i}", [128, IT, MODES], F32)) for i in range(2)]
        raw_ps = [ctx.enter_context(nc.psum_tensor(f"raw_ps{i}", [CI, MODES // 2, MODES], F32)) for i in range(2)]
        raw = pair[:, :, :, 1, :]
        raw_v = raw.rearrange("i (h u) v b -> i h u v b", h=2)
        combined, turned = sem("combined"), sem("turned")
        basis_in, w1_in = sem("basis_in"), sem("w1_in")
        x_in = [sem(f"x_in{t}") for t in range(NX_IN)]
        rows_summed = sem("rows_summed")
        cols_act, cols_dve = sem("cols_act"), sem("cols_dve")
        modes_done = sem("modes_done")
        xh_kept = sem("xh_kept")
        raw_done = sem("raw_done")
        raw_kept = sem("raw_kept")
        block = ctx.enter_context(nc.Block())

        @block.sync
        def _(sp):
            sp.dma_start(basis_h[:], a["basis_h"]).then_inc(basis_in, 16)
            sp.dma_start(basis_w[:], a["basis_w"].rearrange("w (k v) -> w k v", k=4)).then_inc(basis_in, 16)
            sp.dma_start(ident[:], a["ident"][0:MODES, 0:MODES]).then_inc(basis_in, 16)
            for b in range(B):
                for t in range(NL):
                    n = b * NL + t
                    sp.wait_ge(rows_summed, 2 * n + 2)
                    sp.dma_start(xin[:, n % NX_IN], a["x"][b, t * IT:(t + 1) * IT].rearrange("i h w -> h i w"))\
                      .then_inc(x_in[n % NX_IN], 16)
                if b == 1:
                    sp.dma_start(w1[:], a["w1"].rearrange("i o u v -> i o (u v)")).then_inc(w1_in, 16)
            sp.wait_ge(w1_in, 16)

        @block.tensor
        def _(pe):
            pe.sem_inc(rows_summed, 2 * NX_IN)
            pe.sem_inc(modes_done, 2)
            pe.sem_inc(raw_done, 2)
            pe.wait_ge(basis_in, 48)
            with pe.Fori(0, B) as b:
                for half in range(2):
                    for t in range(4 * half, 4 * half + 4):
                        pe.wait_ge(x_in[t % NX_IN], b * (NL // NX_IN * 16) + (t // NX_IN + 1) * 16)
                        for g in range(2):
                            pe.wait_ge((cols_act, cols_dve)[g], b * NL + t + 1)
                            for k in range(4):
                                mm = nc.tensor.matmul(col_ps[2 * (t % 2) + g][:, k, :], xin[:, t % NX_IN, 4 * g + k, :], basis_h[:],
                                                      start=True, stop=True)
                            mm.then_inc(rows_summed, 1)
                    for s in (cols_act, cols_dve):
                        pe.wait_ge(s, b * NL + 4 * half + 6)
                    pe.wait_ge(xh_kept, b * 2 + half + 1)
                    for k in range(4):
                        for t in range(4):
                            mm = nc.tensor.matmul(xh_ps[half][Q * t:Q * t + MODES], basis_w[:, k, :], cols[:, t, :, k, :],
                                                  start=k == 0, stop=k == 3, skip_group_check=True)
                    mm.then_inc(modes_done, 1)
                pe.wait_ge(xh_kept, b * 2 + 4)
                for h in range(2):
                    pe.wait_ge(raw_kept, b * 2 + h + 1)
                    pe.sem_inc(turned, 1)
                    for ul in range(MODES // 2):
                        u = h * (MODES // 2) + ul
                        mm = nc.tensor.transpose(raw_ps[h][:, ul], xh[:, :, :, u].rearrange("v t i -> v (t i)"), ident[:])
                    mm.then_inc(raw_done, 1)

        def copy_cols(copy, eng, b, half, g, kept):
            eng.wait_ge(modes_done, b * 2 + half + 1)
            for t in range(4 * half, 4 * half + 4):
                eng.wait_ge(rows_summed, b * (2 * NL) + 2 * t + g + 1 + 2 * NX_IN)
                copy(cols[:, t % 4, 4 * g:4 * g + 4].rearrange("w i k u -> w i (k u)"),
                     col_ps[2 * (t % 2) + g][:, :, 0:F4]).then_inc(kept, 1)

        @block.scalar
        def _(act):
            act.sem_inc(cols_act, 2)
            act.sem_inc(raw_kept, 2)
            with act.Fori(0, B) as b:
                for half in range(2):
                    copy_cols(nc.scalar.copy, act, b, half, 0, cols_act)
                for h in range(2):
                    act.wait_ge(raw_done, b * 2 + h + 3)
                    dst = raw_v[:, h, :, :, bass.ds(b, 1)].rearrange("i u v b -> i u (v b)")
                    nc.scalar.copy(dst, raw_ps[h][:]).then_inc(raw_kept, 1)

        @block.vector
        def _(dve):
            dve.sem_inc(cols_dve, 2)
            dve.sem_inc(xh_kept, 2)
            with dve.Fori(0, B) as b:
                for half in range(2):
                    copy_cols(nc.vector.tensor_copy, dve, b, half, 1, cols_dve)
                    dve.wait_ge(modes_done, b * 2 + half + 3)
                    if half == 0:
                        dve.wait_ge(raw_done, b * 2 + 2)
                    for t in range(4):
                        last = nc.vector.tensor_copy(xh[:, 4 * half + t], xh_ps[half][Q * t:Q * t + MODES])
                    last.then_inc(xh_kept, 1)
            dve.wait_ge(raw_kept, 2 * B + 2)
            zero, rest, back = slice(0, 1), slice(1, MODES), slice(MODES - 1, 0, -1)
            for u, nu in ((zero, zero), (rest, back)):
                for v, nv in ((zero, zero), (rest, back)):
                    last = nc.vector.tensor_tensor(pair[:, u, v, 0, :], raw[:, nu, nv, :], raw[:, u, v, :], ALU.add)
            last.then_inc(combined, 1)
            dve.wait_ge(combined, 1)
            nc.vector.scalar_tensor_tensor(raw.rearrange("i u v b -> i (u v) b"), raw.rearrange("i u v b -> i (u v) b"), -2.0,
                                           pair[:, :, :, 0, :].rearrange("i u v b -> i (u v) b"), ALU.mult, ALU.add)


def mix(nc, pair, w1):
    with ExitStack() as ctx:
        def sb(name, shape):
            return ctx.enter_context(nc.sbuf_tensor(name, shape, F32))

        def sem(name):
            return ctx.enter_context(nc.semaphore(name))
        w_at = sb("w_at", [CI, 2, MODES, CI])
        sums = sb("sums", [CI, 2, MODES, 2, B])
        mix_ps = [ctx.enter_context(nc.psum_tensor(f"mix_ps{i}", [128, MODES // 2, 2, B], F32)) for i in range(2)]
        at_act, at_dve, sums_ready, mix_begun = map(sem, ("at_act", "at_dve", "sums_ready", "mix_begun"))
        mix_done = sem("mix_done")
        mix_kept = sem("mix_kept")
        block = ctx.enter_context(nc.Block())
        HO = CI // 2

        @block.gpsimd
        def _(pool):
            with pool.Fori(0, MODES // 2) as h:
                for k in range(2):
                    pool.wait_ge(mix_done, 2 * h + k + 1)
                    nc.gpsimd.tensor_copy(sums[:, k].rearrange("i v k b -> i v (k b)"),
                                          pair[:, bass.ds(2 * h + k, 1)].rearrange("i a v k b -> i (a v) (k b)"))\
                      .then_inc(sums_ready, 1)

        @block.scalar
        def _(act):
            with act.Fori(0, MODES // 2) as h:
                for k in range(2):
                    act.wait_ge(mix_done, 2 * h + k + 1)
                    nc.scalar.copy(w_at[:, k, :, 0:HO].rearrange("i v o -> i o v"),
                                   w1[:, 0:HO, bass.ds((2 * h + k) * MODES, MODES)]).then_inc(at_act, 1)

        @block.tensor
        def _(pe):
            pe.sem_inc(mix_done, 2)
            with pe.Fori(0, MODES // 2) as h:
                for k in range(2):
                    pe.wait_ge(at_act, 2 * h + k + 1)
                    pe.wait_ge(at_dve, 2 * h + k + 1)
                    pe.wait_ge(sums_ready, 2 * h + k + 1)
                    pe.wait_ge(mix_kept, 2 * h + k + 1)
                    pe.sem_inc(mix_begun, 1)
                    for v in range(MODES):
                        mm = nc.tensor.matmul(mix_ps[k][(v % 2) * CI:(v % 2 + 1) * CI, v // 2].rearrange("o k b -> o (k b)"),
                                              w_at[:, k, v, :], sums[:, k, v].rearrange("i k b -> i (k b)"),
                                              start=True, stop=True)
                    mm.then_inc(mix_done, 1)

        @block.vector
        def _(dve):
            dve.sem_inc(mix_kept, 2)

            def copy_w(h, k):
                dve.wait_ge(mix_done, 2 * h + k + 1)
                nc.vector.tensor_copy(w_at[:, k, :, HO:CI].rearrange("i v o -> i o v"),
                                      w1[:, HO:CI, bass.ds((2 * h + k) * MODES, MODES)]).then_inc(at_dve, 1)

            def keep(h, k):
                dve.wait_ge(mix_done, 2 * h + k + 3)
                for odd in range(2):
                    last = nc.vector.tensor_copy(
                        pair[:, bass.ds(2 * h + k, 1), odd::2, :, :].rearrange("o a v k b -> o (a v) (k b)"),
                        mix_ps[k][odd * CI:(odd + 1) * CI].rearrange("o v k b -> o v (k b)"))
                last.then_inc(mix_kept, 1)

            copy_w(0, 0)
            copy_w(0, 1)
            with dve.Fori(0, MODES // 2 - 1) as h:
                for k in range(2):
                    keep(h, k)
                    copy_w(h + 1, k)
            keep(MODES // 2 - 1, 0)
            keep(MODES // 2 - 1, 1)
            dve.wait_ge(mix_kept, MODES + 2)
            zero, rest, back = slice(0, 1), slice(1, MODES), slice(MODES - 1, 0, -1)
            for u, nu in ((zero, zero), (rest, back)):
                for v, nv in ((zero, zero), (rest, back)):
                    nc.vector.tensor_tensor(pair[:, u, v, 0, :], pair[:, u, v, 0, :], pair[:, nu, nv, 1, :], ALU.add)


def smooth(nc, a, gauss, pair, modes):
    with ExitStack() as ctx:
        def sb(name, shape):
            return ctx.enter_context(nc.sbuf_tensor(name, shape, F32))

        def sem(name):
            return ctx.enter_context(nc.semaphore(name))
        sm_c = sb("sm_c_sb", [CI, NFAST])
        padded = sb("padded", [KP, KC, B + 2 * R, CI])
        ps = [ctx.enter_context(nc.psum_tensor(f"chan_ps{i}", [128, 4, 128], F32)) for i in range(8)]
        smc_in, chan_done, kept_act, kept_dve, padding, step = map(
            sem, ("smc_in", "chan_done", "kept_act", "kept_dve", "padding", "smooth_step"))
        mixed = pair[:].rearrange("o u v k b -> o (u v) k b")
        block = ctx.enter_context(nc.Block())

        @block.sync
        def _(sp):
            sp.dma_start(sm_c[:], a["sm_c"]).then_inc(smc_in, 16)

        @block.tensor
        def _(pe):
            pe.wait_ge(smc_in, 16)
            for n in range(4 * KC):
                if n >= 8:
                    pe.wait_ge((kept_act, kept_dve)[n % 2], (n - 8) // 2 + 1)
                for b in range(4):
                    mm = nc.tensor.matmul(ps[n % 8][0:KP, b, 0:NFAST],
                                          mixed[:, (n // 4) * KP:(n // 4 + 1) * KP, 0, 4 * (n % 4) + b],
                                          sm_c[:], start=True, stop=True)
                mm.then_inc(chan_done, 1)

        def keep(copy, eng, kept, n):
            eng.wait_ge(chan_done, n + 1)
            b0 = R + 4 * (n % 4)
            copy(padded[:, n // 4, b0:b0 + 4, :], ps[n % 8][0:KP, :, 0:CI]).then_inc(kept, 1)

        @block.scalar
        def _(act):
            for n in range(0, 4 * KC, 2):
                keep(nc.scalar.copy, act, kept_act, n)

        @block.vector
        def _(dve):
            for n in range(1, 4 * KC, 2):
                keep(nc.vector.tensor_copy, dve, kept_dve, n)
            dve.wait_ge(kept_act, 2 * KC)
            dve.wait_ge(kept_dve, 2 * KC)
            for edge, own in ((slice(0, R), R), (slice(B + R, B + 2 * R), B + R - 1)):
                nc.vector.tensor_copy(padded[:, :, edge, :],
                                      padded[:, :, own, :].unsqueeze(2).broadcast_to([KP, KC, R, CI])).then_inc(padding, 1)
            dve.wait_ge(padding, 2)

            def at(t):
                return padded[:, :, t:t + B, :].rearrange("m k b o -> m k (b o)")
            nc.vector.tensor_scalar(modes[:], at(0), gauss[0], None, ALU.mult).then_inc(step, 1)
            for t in range(1, 2 * R + 1):
                dve.wait_ge(step, t)
                nc.vector.scalar_tensor_tensor(modes[:], at(t), gauss[t], modes[:], ALU.mult, ALU.add).then_inc(step, 1)


def coefs(nc, a, modes, win_t, bias_f, coef_d):
    NCH = 2 * len(LIVE)
    PIECE = 4 * 2 * PF
    QN = 2
    NY, NC = QN * NCH, 4 * QN * NCH
    STEPS = B // (2 * QN)
    with ExitStack() as ctx:
        def sb(name, shape):
            return ctx.enter_context(nc.sbuf_tensor(name, shape, F32))

        def sem(name):
            return ctx.enter_context(nc.semaphore(name))
        synth = sb("synth_sb", [KP, 2, KC, PIECE])
        now = sb("now", [KP, KC, QN * 128])
        y = sb("y", [128, QN, NCH, PIECE])
        st = [sb(f"coef_st{h}", [128, 128, NS, NJ]) for h in range(CH)]
        y_ps = [ctx.enter_context(nc.psum_tensor(f"y_ps{i}", [128, PIECE], F32)) for i in range(4)]
        c_ps = [ctx.enter_context(nc.psum_tensor(f"c_ps{i}", [128, 4, 128], F32)) for i in range(4)]
        synth_in = [sem(f"synth_in{i}") for i in range(2)]
        stored = [sem(f"coef_stored{i}") for i in range(CH)]
        st_free = [sem(f"st_free{i}") for i in range(CH)]
        now_ready = sem("now_ready")
        y_done = sem("y_done")
        y_kept = sem("y_kept")
        c_done = sem("c_done")
        c_kept = sem("c_kept")
        const_set = sem("const_set")
        block = ctx.enter_context(nc.Block())

        @block.sync
        def _(sp):
            with sp.Fori(0, STEPS) as i:
                for n in range(NCH):
                    sp.wait_ge(y_done, i * NY + QN * (n - 1) + NY)
                    sp.dma_start(synth[:, n % 2], a["synth"][n].rearrange("m (k p) -> m k p", k=KC)).then_inc(synth_in[n % 2], 16)

        @block.gpsimd
        def _(pool):
            with pool.Fori(0, STEPS) as i:
                for e in range(2 * QN):
                    for h in range(CH):
                        pool.wait_ge(c_kept, i * NC + (2 * e + h + 1) * NCH + 4)
                        pool.dma_start(coef_d[bass.ds(2 * QN * i + e, 1), h].rearrange("b p n -> p (b n)"),
                                       st[h][:].rearrange("p c s j -> p (c s j)")).then_inc(stored[h], 16)
                        if (e, h) != (0, 0):
                            pool.wait_ge(stored[1 - h], i * (2 * QN * 16) + (e + h) * 16)
                            pool.sem_inc(st_free[1 - h], 1)
                pool.wait_ge(stored[CH - 1], (i + 1) * (2 * QN * 16))
                pool.sem_inc(st_free[CH - 1], 1)

        @block.tensor
        def _(pe):
            pe.sem_inc(y_done, NY)
            pe.sem_inc(c_done, NC)
            with pe.Fori(0, STEPS) as i:
                pe.wait_ge(now_ready, i + 1)
                for n in range(NCH):
                    pe.wait_ge(synth_in[n % 2], i * 16 * (NCH // 2) + 16 * (n // 2) + 16)
                    for q in range(QN):
                        m = QN * n + q
                        pe.wait_ge(y_kept, i * NY + m + 1)
                        for k in range(KC):
                            mm = nc.tensor.matmul(y_ps[m % 4][:], now[:, k, q * 128:(q + 1) * 128], synth[:, n % 2, k, :],
                                                  start=k == 0, stop=k == KC - 1)
                        mm.then_inc(y_done, 1)
                pe.wait_ge(y_kept, (i + 1) * NY + 4)
                for e in range(2 * QN):
                    for h in range(CH):
                        for n in range(NCH):
                            m = (2 * e + h) * NCH + n
                            pe.wait_ge(c_kept, i * NC + m + 1)
                            for j in range(4):
                                mm = nc.tensor.matmul(c_ps[m % 4][:, j, :], y[:, e // 2, n, j * 128:(j + 1) * 128],
                                                      win_t[:, e % 2, h * 128:(h + 1) * 128], start=True, stop=True)
                            mm.then_inc(c_done, 1)

        @block.scalar
        def _(act):
            act.sem_inc(y_kept, 4)
            with act.Fori(0, STEPS) as i:
                act.wait_ge(y_done, i * NY + NY)
                nc.scalar.copy(now[:], modes[:, :, bass.ds(i * (QN * 128), QN * 128)]).then_inc(now_ready, 1)
                act.wait_ge(c_done, (i + 1) * NC)
                for m in range(NY):
                    act.wait_ge(y_done, i * NY + m + 1 + NY)
                    nc.scalar.copy(y[:, m % QN, m // QN, :], y_ps[m % 4][:]).then_inc(y_kept, 1)

        @block.vector
        def _(dve):
            dve.sem_inc(c_kept, 4)
            for h in range(CH):
                dve.sem_inc(st_free[h], 1)
            for h in range(CH):
                for s in range(CONST0, CONST0 + NCONST):
                    for j in range(0, NJ, 4):
                        nc.vector.tensor_copy(st[h][:, :, s, j:j + 4].rearrange("p c j -> p j c"), bias_f[:, h])\
                          .then_inc(const_set, 1)
            with dve.Fori(0, STEPS) as i:
                for e in range(2 * QN):
                    for h in range(CH):
                        dve.wait_ge(st_free[h], 2 * QN * i + e + 1)
                        for n in range(NCH):
                            m = (2 * e + h) * NCH + n
                            dve.wait_ge(c_done, i * NC + m + 1 + NC)
                            j = 4 * (n % 2)
                            nc.vector.tensor_tensor(st[h][:, :, SLOT[n // 2], j:j + 4].rearrange("p c j -> p j c"),
                                                    c_ps[m % 4][:], bias_f[:, h], ALU.add).then_inc(c_kept, 1)


def conv(nc, op_d, coef_d, z_d):
    NCB = C // CB
    BG = 4
    NG = B // BG
    PER = CB * NG
    ZR = 4
    LAST = NCB // 2 - 1
    with ExitStack() as ctx:
        def sb(name, shape):
            return ctx.enter_context(nc.sbuf_tensor(name, shape, F32))

        def sem(name):
            return ctx.enter_context(nc.semaphore(name))
        xs = [sb(f"xs{i}", [128, B, CB, NX]) for i in range(2)]
        xsh = [sb(f"xsh{i}", [128, B, CB, NS, NJ + 1]) for i in range(2)]
        op = [sb(f"op{i}", [128, 2, CB, PF]) for i in range(2)]
        z = sb("z_st", [128, ZR, B, NT, NJ])
        z_top = sb("z_top", [32, ZR, B, NT, NJ])
        ps = [ctx.enter_context(nc.psum_tensor(f"z_ps{i}", [128, 512], F32)) for i in range(8)]
        xs_in = [sem(f"xs_in{i}") for i in range(2)]
        op_in = [sem(f"op_in{i}") for i in range(2)]
        stored = [sem(f"z_stored{i}") for i in range(ZR)]
        z_done = sem("z_done")
        z_act, z_dve = sem("z_act"), sem("z_dve")
        up_done, down_done = sem("up_done"), sem("down_done")
        zero_set = sem("zero_set")
        block = ctx.enter_context(nc.Block())

        @block.sync
        def _(sp):
            for r in range(ZR):
                sp.sem_inc(stored[r], 32)

            def load(i, k):
                sp.wait_ge(z_done, i * (2 * PER) + (k + 1) * PER)
                sp.dma_start(xs[k][:].rearrange("p b c n -> p b (c n)"),
                             coef_d[:, k, :, bass.ds(i * (CB * NX), CB * NX)].rearrange("b p n -> p b n"))\
                  .then_inc(xs_in[k], 16)
                sp.dma_start(op[k][:].rearrange("p s c o -> p (s c o)"),
                             op_d[:, bass.ds(i + k * (NCB // 2), 1)].rearrange("p n s c o -> p (n s c o)")).then_inc(op_in[k], 16)

            def store(i, k):
                for c in range(CB):
                    r = c % ZR
                    for kept in (z_act, z_dve):
                        sp.wait_ge(kept, i * (2 * CB * 4) + 4 * (k * CB + c) + 12)
                    dst = z_d[bass.ds(i * CB + k * 128 + c, 1)].rearrange("c p b n -> (c p) b n")
                    sp.dma_start(dst[0:32], z_top[:, r].rearrange("p b t j -> p b (t j)")).then_inc(stored[r], 16)
                    sp.dma_start(dst[32:128], z[32:128, r].rearrange("p b t j -> p b (t j)")).then_inc(stored[r], 16)

            load(0, 0)
            load(0, 1)
            with sp.Fori(0, LAST) as i:
                store(i, 0)
                load(i + 1, 0)
                store(i, 1)
                load(i + 1, 1)
            store(LAST, 0)
            store(LAST, 1)
            for r in range(ZR):
                sp.wait_ge(stored[r], 32 * (C // ZR) + 32)

        @block.tensor
        def _(pe):
            pe.sem_inc(z_done, 2 * PER)
            with pe.Fori(0, NCB // 2) as i:
                for k in range(2):
                    pe.wait_ge(op_in[k], i * 16 + 16)
                    pe.wait_ge(xs_in[k], i * 16 + 16)
                    for c in range(CB):
                        cl = k * CB + c
                        pe.wait_ge(up_done, i * (2 * CB) + cl + 1)
                        pe.wait_ge(down_done, i * (2 * CB) + cl + 1)
                        for g in range(NG):
                            pe.wait_ge((z_act, z_dve)[g % 2], i * (2 * CB * 4) + 4 * cl + 2 * (g // 2) + 2)
                            tile = ps[(cl * NG + g) % 8][:, 0:BG * NT * (NJ + 1)].rearrange("p (b t j) -> p b t j", b=BG, t=NT)
                            bs = slice(g * BG, (g + 1) * BG)
                            nat = xs[k][:, bs, c, :].rearrange("p b (s j) -> p b s j", s=NS)
                            for side, ts in ((0, slice(1, NT)), (1, slice(0, NS))):
                                nc.tensor.matmul(tile[0:PF, :, ts, :], op[k][:, side, c, :], xsh[k][:, bs, c],
                                                 start=side == 0, stop=side == 1, skip_group_check=True)
                                mm = nc.tensor.matmul(tile[PF:128, :, ts, 0:NJ], op[k][:, side, c, :], nat,
                                                      start=side == 0, stop=side == 1, skip_group_check=True)
                            mm.then_inc(z_done, 1)

        def shift(copy, eng, i, k, c, done, up):
            if c == 0:
                eng.wait_ge(xs_in[k], i * 16 + 16)
            nat = xs[k][:, :, c, :].rearrange("p b (s j) -> p b s j", s=NS)
            if up:
                copy(xsh[k][0:PF, :, c, :, 1:NJ + 1], nat[PF:128]).then_inc(done, 1)
            else:
                copy(xsh[k][PF:128, :, c, :, 0:NJ], nat[0:PF]).then_inc(done, 1)

        def evacuate(copy, eng, kept, done, up):
            def of_load(i, k, following):
                for c in range(CB):
                    cl = k * CB + c
                    r = cl % ZR
                    eng.wait_ge(stored[r], i * (2 * CB // ZR * 32) + 32 * (cl // ZR) + 32)
                    for g in ((0, 2) if up else (1, 3)):
                        tile = ps[(cl * NG + g) % 8][:, 0:BG * NT * (NJ + 1)].rearrange("p (b t j) -> p b t j", b=BG, t=NT)
                        bs = slice(g * BG, (g + 1) * BG)
                        eng.wait_ge(z_done, i * (2 * PER) + cl * NG + g + 1 + 2 * PER)
                        copy(z[:, r, bs], tile[:, :, :, 0:NJ]).then_inc(kept, 1)
                        copy(z_top[:, r, bs], tile[0:32, :, :, 1:NJ + 1]).then_inc(kept, 1)
                    if following:
                        shift(copy, eng, *following, c, done, up)

            for c in range(CB):
                shift(copy, eng, 0, 0, c, done, up)
            with eng.Fori(0, LAST) as i:
                of_load(i, 0, (i, 1))
                of_load(i, 1, (i + 1, 0))
            of_load(LAST, 0, (LAST, 1))
            of_load(LAST, 1, None)

        @block.scalar
        def _(act):
            act.sem_inc(z_act, 8)
            act.wait_ge(zero_set, 4)
            evacuate(nc.scalar.copy, act, z_act, up_done, True)

        @block.vector
        def _(dve):
            dve.sem_inc(z_dve, 8)
            for k in range(2):
                nc.vector.memset(xsh[k][0:PF, :, :, :, 0], 0.0).then_inc(zero_set, 1)
                nc.vector.memset(xsh[k][PF:128, :, :, :, NJ], 0.0).then_inc(zero_set, 1)
            dve.wait_ge(zero_set, 4)
            evacuate(nc.vector.tensor_copy, dve, z_dve, down_done, False)


def project(nc, z_d, wout_t, bdw, bout, out):
    PX = 8
    NL = 2 * P
    ZB = 4
    with ExitStack() as ctx:
        def sb(name, shape):
            return ctx.enter_context(nc.sbuf_tensor(name, shape, F32))

        def sem(name):
            return ctx.enter_context(nc.semaphore(name))
        zt = [sb(f"zt{i}", [128, CH, PX, 2, NZ]) for i in range(ZB)]
        img = [sb(f"img{i}", [128, H, W]) for i in range(2)]
        ps = [ctx.enter_context(nc.psum_tensor(f"o_ps{i}", [128, 512], F32)) for i in range(8)]
        z_in = [sem(f"z_in{i}") for i in range(ZB)]
        stored = sem("img_stored")
        img_free = [sem(f"img_free{i}") for i in range(2)]
        act_done = sem("gelu_done")
        o_done = sem("o_done")
        o_kept = sem("o_kept")
        block = ctx.enter_context(nc.Block())
        z_v = z_d.rearrange("(h c) x b n -> c h x b n", h=CH)

        @block.sync
        def _(sp):
            with sp.Fori(0, B // 4) as i:
                for k in range(2):
                    for n in range(NL):
                        m = k * NL + n
                        sp.wait_ge(o_done, i * (4 * NL) + 2 * m + 2)
                        for h in range(CH):
                            src = z_v[:, h, n * PX:(n + 1) * PX, bass.ds(4 * i + 2 * k, 2)]
                            sp.dma_start(zt[m % ZB][:, h], src).then_inc(z_in[m % ZB], 16)

        @block.gpsimd
        def _(pool):
            with pool.Fori(0, B // 4) as i:
                for k in range(2):
                    pool.wait_ge(o_kept, i * (4 * NL) + (k + 1) * 2 * NL + 8)
                    pool.dma_start(out[bass.ds(4 * i + 2 * k, 2)].rearrange("b o h w -> (b o) (h w)"),
                                   img[k][:].rearrange("p h w -> p (h w)")).then_inc(stored, 16)
                    pool.wait_ge(stored, i * 32 + 16 * (k + 1))
                    pool.sem_inc(img_free[k], 1)

        @block.scalar
        def _(act):
            with act.Fori(0, B // 4) as i:
                for m in range(2 * NL):
                    act.wait_ge(z_in[m % ZB], i * (2 * NL // ZB * 32) + 32 * (m // ZB) + 32)
                    for h in range(CH):
                        v = zt[m % ZB][:, h].rearrange("c x b n -> c (x b n)")
                        nc.scalar.activation(v, v, ACT.Gelu, bias=bdw[:, h:h + 1]).then_inc(act_done, 1)

        @block.tensor
        def _(pe):
            pe.sem_inc(o_done, 2 * ZB)
            with pe.Fori(0, B // 4) as i:
                for m in range(2 * NL):
                    pe.wait_ge(act_done, i * (4 * NL) + 2 * m + 2)
                    for q in range(2):
                        n = 2 * m + q
                        pe.wait_ge(o_kept, i * (4 * NL) + n + 1)
                        for h in range(CH):
                            for e in range(2):
                                mm = nc.tensor.matmul(ps[n % 8][e * CI:(e + 1) * CI, 0:4 * NZ].rearrange("o (x n) -> o x n", x=4),
                                                      wout_t[:, h, :], zt[m % ZB][:, h, 4 * q:4 * q + 4, e, :],
                                                      start=h == 0, stop=h == CH - 1)
                        mm.then_inc(o_done, 1)

        @block.vector
        def _(dve):
            dve.sem_inc(o_kept, 8)
            for k in range(2):
                dve.sem_inc(img_free[k], 1)
            with dve.Fori(0, B // 4) as i:
                for k in range(2):
                    dve.wait_ge(img_free[k], i + 1)
                    for n in range(NL):
                        first = n - P // 2 if n >= P // 2 else n - P // 2 + 2 * P
                        rows = img[k][:, first::2 * P, :]
                        groups = rows.rearrange("p j (g x) -> p x g j", x=4)
                        for q in range(2):
                            m = 2 * (k * NL + n) + q
                            dve.wait_ge(o_done, i * (4 * NL) + m + 1 + 2 * ZB)
                            src = ps[m % 8][:, 0:4 * NZ].rearrange("p (x t j) -> p x t j", x=4, t=NT)
                            if q == 0:
                                pieces = ((slice(1, 6), groups[:, :, 1:11:2, :]), (slice(7, 12), groups[:, :, 23:32:2, :]))
                            else:
                                pieces = ((slice(0, 6), groups[:, :, 0:12:2, :]), (slice(7, 11), groups[:, :, 24:32:2, :]))
                            for ts, dst in pieces:
                                last = nc.vector.tensor_scalar(dst, src[:, :, ts, :], bout[:, 0:1], None, ALU.add)
                                if q == 0 and ts.start == 1:
                                    mid = src[:, 0, 6, :].unsqueeze(2).broadcast_to([128, NJ, MID1 - MID0])
                                    nc.vector.tensor_scalar(rows[:, :, MID0:MID1], mid, bout[:, 0:1], None, ALU.add)
                            last.then_inc(o_kept, 1)


NAMES = {"x": "x", "w1": "L0_conv_w1", "w_in": "L1_conv_w_in", "b_in": "L1_conv_b_in",
         "fft_filter": "L1_conv_fft_filter", "w_dw": "L1_conv_w_dw", "b_dw": "L1_conv_b_dw",
         "w_out": "L1_conv_w_out", "b_out": "L1_conv_b_out"}
DEBUG = False


def kernel(**inputs):
    import numpy as np
    import concourse.bacc as bacc
    from concourse.bass_utils import run_bass_kernel_spmd

    nc = bacc.Bacc("TRN2", target_bir_lowering=False, num_devices=1)
    arrays, aps = {}, {}
    tables, gauss = constants()
    given = {k: np.ascontiguousarray(inputs[v]) for k, v in NAMES.items()}
    for k in ("w_in", "w_out"):
        given[k] = given[k].reshape(given[k].shape[:2])
    for k in ("fft_filter", "w_dw"):
        given[k] = given[k].reshape(C, -1)
    for k, v in {**given, **tables}.items():
        arrays[f"in_{k}"] = v
        aps[k] = nc.dram_tensor(f"in_{k}", v.shape, F32, kind="ExternalInput").ap()
    out = nc.dram_tensor("out", (B, CI, H, W), F32, kind="ExternalOutput").ap()
    build(nc, aps, gauss, out, DEBUG)
    r = run_bass_kernel_spmd(nc, [arrays], core_ids=[0])
    return r.results[0]["out"]
```

```python
from contextlib import ExitStack
from itertools import accumulate

import concourse.bass as bass
from concourse import mybir

F32 = mybir.dt.float32
ACT = mybir.ActivationFunctionType
ALU = mybir.AluOpType

B, CI, H, W = 16, 64, 128, 128
C = 256
CH = C // 128
MODES = 20
NM = MODES * MODES
KC, KP = 4, NM // 4
P = 8
PF = P * P
NJ = H // (2 * P)
R = 4
TAPS = 7
LIVE = [0, 1, 2, 3, 4, 12, 13, 14, 15]
SLOT = [0, 1, 2, 3, 4, 6, 7, 8, 9]
CONST = 5
NS = len(LIVE) + 1
NT = NS + 1
NX = NS * NJ
NZ = NT * NJ
CB = 4
BI = 8
NFAST = 96
MID0, MID1 = 44, 92


def constants():
    import numpy as np
    th = 2 * np.pi / W
    t = np.arange(-R, R + 1, dtype=np.float32)
    g = np.exp(-0.5 * t ** 2)
    g = (g / g.sum()).astype(np.float64)

    def smooth(n):
        m = np.zeros((n, n))
        for i in range(n):
            for k in range(2 * R + 1):
                m[i, min(max(i + k - R, 0), n - 1)] += g[k]
        return m

    u = np.arange(MODES)
    p = np.arange(H)
    c0, s0 = np.cos(th * np.outer(p, u)), np.sin(th * np.outer(p, u))
    c1, s1 = np.cos(th * np.outer(p + 1, u)), np.sin(th * np.outer(p + 1, u))
    basis_h = np.concatenate([c0, s0, c1, s1, np.zeros((H, NFAST - 4 * MODES))], 1)
    basis_w = np.stack([c0, -s0, -s1, -c1], 1)
    ident = np.eye(128)
    sm_c = np.concatenate([smooth(CI).T, np.zeros((CI, NFAST - CI))], 1)
    sh = smooth(H)
    mask = (np.abs(np.fft.fftfreq(W)) <= 0.25).astype(np.float64)
    sw = mask[:, None] * smooth(W)
    cu, su = np.cos(th * np.outer(p, u + 1)), np.sin(th * np.outer(p, u + 1))
    rows = [sh @ c0, -(sh @ s0), -(sh @ su), -(sh @ cu)]
    cols = [sw @ c0, sw @ s0, sw @ cu, sw @ su]
    funcs, lam = [], []
    yy, xx = np.meshgrid(np.arange(P), np.arange(P), indexing="ij")
    nk = P // 2 + 1
    for kx in range(nk):
        edge = kx in (0, P // 2)
        for ky in range(P):
            if edge and ky > P // 2:
                continue
            a = 2 * np.pi * (ky * yy + kx * xx) / P
            w = np.zeros((P, nk))
            if edge:
                w[ky, kx] += 0.5
                w[(-ky) % P, kx] += 0.5
            else:
                w[ky, kx] = 1.0
            own = edge and ky in (0, P // 2)
            n = (1.0 if own else np.sqrt(2.0)) / P
            funcs.append(np.cos(a).ravel() * n)
            lam.append(w.ravel())
            if not own:
                funcs.append(np.sin(a).ravel() * n)
                lam.append(w.ravel())
    v = np.array(funcs)
    assert v.shape == (PF, PF) and np.allclose(v @ v.T, np.eye(PF))
    lam = np.array(lam).T
    v3 = v.reshape(PF, P, P)
    rr = np.stack(rows).reshape(4, H // P, P, MODES)
    cc = np.stack(cols).reshape(4, W // P, P, MODES)[:, LIVE]
    a1 = np.einsum("fyx,ksxv->ksfyv", v3, cc)
    tab = np.zeros((len(LIVE), MODES, MODES, H // P, PF))
    for k in range(4):
        for r in range(H // P):
            tab[:, :, :, r, :] += np.einsum("yu,sfyv->suvf", rr[k, r], a1[k], optimize=True)
    tab *= 0.5 / (H * W)
    tab = tab.reshape(len(LIVE), KC, KP, 2, 4 * 2 * PF).transpose(0, 3, 2, 1, 4)
    synth = tab.reshape(len(LIVE) * 2, KP, KC * 4 * 2 * PF)
    taps = np.zeros((TAPS, TAPS, 2, P, P, 2, PF))
    for dy in range(TAPS):
        for dx in range(TAPS):
            for y in range(P):
                my = y - P // 2 + dy - TAPS // 2
                role, ry = (1, my) if my >= 0 else (0, my + P)
                for x in range(P):
                    mx = x - P // 2 + dx - TAPS // 2
                    side, rx = (1, mx) if mx >= 0 else (0, mx + P)
                    taps[dy, dx, side, y, x, role] = v3[:, ry, rx]
    taps = taps.reshape(TAPS * TAPS, 2 * PF * 2 * PF)
    eight = np.zeros((1, 128))
    eight[0, 0] = eight[0, PF] = float(P)
    out = dict(basis_h=basis_h, basis_w=basis_w.reshape(W, 4 * MODES), ident=ident,
               sm_c=sm_c, lam=np.concatenate([lam, lam], 1), synth=synth, taps=taps, eight=eight)
    return {k: np.ascontiguousarray(a, dtype=np.float32) for k, a in out.items()}, [float(a) for a in g]


def build(nc, a, gauss, out):
    op_d = nc.dram_tensor("op_scratch", (128, 2, C, PF), F32, kind="Internal").ap()
    coef_d = nc.dram_tensor("coef_scratch", (B, CH, 128, 128 * NX), F32, kind="Internal").ap()
    z_d = nc.dram_tensor("z_scratch", (C, 128, B, NZ), F32, kind="Internal").ap()
    with ExitStack() as keep:
        def sb(name, shape):
            return keep.enter_context(nc.sbuf_tensor(name, shape, F32))
        win_t = sb("win_t", [128, 2, C])
        wout_t = sb("wout_t", [128, CH, CI])
        bias_f = sb("bias_f", [128, CH, 4, 128])
        bdw = sb("bdw", [128, CH])
        bout = sb("bout", [128, 1])
        with nc.sbuf_tensor("padded", [128, KC, (B + 2 * R) * CI], F32) as whole:
            padded = whole[0:KP]
            with nc.sbuf_tensor("region", [128, CI * NM], F32) as region:
                operators(nc, a, op_d, region, win_t, wout_t, bias_f, bdw, bout)
                with nc.sbuf_tensor("pair", [128, MODES, MODES, 2, B], F32) as pair:
                    w1 = region[0:CI].rearrange("i (o m) -> i o m", o=CI)
                    analyse(nc, a, pair, w1, whole, region, op_d)
                    mix(nc, pair[0:CI], w1)
                    smooth(nc, a, pair, padded)
            coefs(nc, a, gauss, padded, win_t, bias_f, coef_d)
        mid = sb("mid", [128, CH, 2 * P, NJ])
        mid_out = sb("mid_out", [128, 2 * P, NJ])
        conv(nc, a, op_d, coef_d, z_d, mid, mid_out, wout_t, bdw, bout, out)


def operators(nc, a, op_d, region, win_t, wout_t, bias_f, bdw, bout):
    with ExitStack() as ctx:
        def sb(name, shape):
            return ctx.enter_context(nc.sbuf_tensor(name, shape, F32))

        def sem(name):
            return ctx.enter_context(nc.semaphore(name))
        ident = sb("ident", [128, 128])
        win = sb("win", [128, CH, CI])
        wout = sb("wout", [CI, C])
        wdw = sb("wdw", [128, CH, TAPS * TAPS])
        filt = sb("filt", [128, CH, P * (P // 2 + 1)])
        lam_m = sb("lam_m", [P * (P // 2 + 1), 128])
        eight = sb("eight_sb", [1, 128])
        bin_row = sb("bin_row", [1, C])
        wdw_t = sb("wdw_t", [128, C])
        filt_t = sb("filt_t", [P * (P // 2 + 1), C])
        lam = sb("lam_sb", [128, 2, C])
        ops = [sb("ops0", [128, C, PF])[:], region[:, 0:C * PF].rearrange("p (c o) -> p c o", c=C)]
        taps = region[:, C * PF:C * PF + PF * 128].rearrange("p (a o m) -> p a o m", a=2, m=128)
        ps = [ctx.enter_context(nc.psum_tensor(f"op_ps{i}", [128, 2, C], F32)) for i in range(8)]
        weights_in, taps_in0, trans_done, trans_kept, lam_done, lam_kept = map(
            sem, ("weights_in", "taps_in0", "trans_done", "trans_kept", "lam_done", "lam_kept"))
        op_done, op_kept, op0_stored = map(sem, ("op_done", "op_kept", "op0_stored"))
        taps_v = a["taps"].rearrange("t (q o s) -> q t o s", q=4, s=128)
        zeroed = sem("zeroed")
        NSMALL = 11
        taps_in = (taps_in0, sem("taps_in1"))
        block = ctx.enter_context(nc.Block())

        @block.sync
        def _(sp):
            for dst, src in (
                (ident[:], a["ident"]),
                (win[:], a["w_in"].rearrange("(h c) i -> c h i", h=CH)),
                (wout[:], a["w_out"]),
                (wdw[:], a["w_dw"].rearrange("(h c) t -> c h t", h=CH)),
                (filt[:], a["fft_filter"].rearrange("(h c) k -> c h k", h=CH)),
                (lam_m[:], a["lam"]),
                (eight[:], a["eight"]),
                (bin_row[:], a["b_in"].rearrange("(a c) -> a c", a=1)),
                (bdw[:], a["b_dw"].rearrange("(h c) -> c h", h=CH)),
                (bout[0:CI, :], a["b_out"].rearrange("(o a) -> o a", a=1)),
                (bout[CI:128, :], a["b_out"].rearrange("(o a) -> o a", a=1)),
            ):
                with nc.allow_non_contiguous_dma(reason="a few hundred words, once"):
                    sp.dma_start(dst, src).then_inc(weights_in, 16)
            sp.wait_ge(op_kept, 32)
            sp.dma_start(op_d[:, 0].rearrange("p c o -> p (c o)"), ops[0].rearrange("p c o -> p (c o)")).then_inc(op0_stored, 16)
            sp.wait_ge(op0_stored, 16)

        @block.gpsimd
        def _(pool):
            pool.wait_ge(zeroed, 3)
            for q in range(4):
                if q >= 2:
                    pool.wait_ge(op_done, 16 * (q - 1))
                pool.dma_start(taps[0:TAPS * TAPS, q % 2], taps_v[q]).then_inc(taps_in[q % 2], 16)

        @block.tensor
        def _(pe):
            pe.wait_ge(weights_in, 16 * NSMALL)
            for h in range(CH):
                cs = slice(128 * h, 128 * (h + 1))
                for e in range(2):
                    nc.tensor.matmul(ps[0][e * CI:(e + 1) * CI, 0, cs], win[:, h, :], ident[:], start=True, stop=True)
                nc.tensor.matmul(ps[1][:, 0, h * CI:(h + 1) * CI], wout[:, cs], ident[0:CI, 0:CI], start=True, stop=True)
                nc.tensor.matmul(ps[2][0:TAPS * TAPS, 0, cs], wdw[:, h, :], ident[:], start=True, stop=True)
                nc.tensor.matmul(ps[3][0:P * (P // 2 + 1), 0, cs], filt[:, h, :], ident[:], start=True, stop=True)
            nc.tensor.matmul(ps[4][:, 0, :], eight[:], bin_row[:], start=True, stop=True).then_inc(trans_done, 1)
            pe.wait_ge(trans_kept, 7)
            for k in range(2):
                nc.tensor.matmul(ps[5][:, k, :], lam_m[:], filt_t[:], start=True, stop=True).then_inc(lam_done, 1)
            for half in range(2):
                for q in range(32):
                    n = 32 * half + q
                    if n % 16 == 0:
                        pe.wait_ge(taps_in[n // 16 % 2], 16 * (n // 32 + 1))
                    if n >= 8:
                        pe.wait_ge(op_kept, n - 7)
                    elif n == 5:
                        pe.wait_ge(lam_kept, 1)
                    for k in range(2):
                        mm = nc.tensor.matmul(ps[n % 8][:, k, :], taps[:, n // 16 % 2, 2 * (n % 16) + k, :], wdw_t[:], start=True, stop=True)
                    mm.then_inc(op_done, 1)

        @block.vector
        def _(dve):
            for q in range(2):
                nc.vector.memset(taps[:, q], 0.0).then_inc(zeroed, 1)
            nc.vector.memset(wdw_t[:], 0.0).then_inc(zeroed, 1)
            dve.wait_ge(zeroed, 3)
            dve.wait_ge(trans_done, 1)
            nc.vector.memset(win_t[:], 0.0).then_inc(trans_kept, 1)
            dve.wait_ge(trans_kept, 1)
            for dst, src in ((win_t[0:CI, 0, :], ps[0][0:CI, 0, :]),
                             (win_t[CI:128, 1, :], ps[0][CI:128, 0, :]),
                             (wout_t[:], ps[1][:, 0, 0:CH * CI].rearrange("c (h o) -> c h o", h=CH)),
                             (wdw_t[0:TAPS * TAPS, :], ps[2][0:TAPS * TAPS, 0, :]),
                             (filt_t[:], ps[3][0:P * (P // 2 + 1), 0, :])):
                nc.vector.tensor_copy(dst, src).then_inc(trans_kept, 1)
            for j in range(4):
                last = nc.vector.tensor_copy(bias_f[:, :, j, :], ps[4][:, 0, :].rearrange("p (h c) -> p h c", h=CH))
            last.then_inc(trans_kept, 1)
            dve.wait_ge(lam_done, 2)
            nc.vector.tensor_copy(lam[:], ps[5][:]).then_inc(lam_kept, 1)
            dve.wait_ge(lam_kept, 1)
            for n in range(64):
                dve.wait_ge(op_done, n + 1)
                q = n % 32
                nc.vector.tensor_tensor(ops[n // 32][:, :, 2 * q:2 * q + 2].rearrange("p c k -> p k c"), ps[n % 8][:],
                                        lam[:], ALU.mult).then_inc(op_kept, 1)


def analyse(nc, a, pair, w1, space, region, op_d):
    IT = 8
    NL = CI // IT
    NX_IN = 4
    F4 = 4 * MODES
    Q = 32
    with ExitStack() as ctx:
        def sb(name, shape):
            return ctx.enter_context(nc.sbuf_tensor(name, shape, F32))

        def sem(name):
            return ctx.enter_context(nc.semaphore(name))
        xin = space[:].rearrange("p k n -> p (k n)")[:, 0:NX_IN * IT * W].rearrange("p (l i w) -> p l i w", l=NX_IN, i=IT)
        basis_h = sb("basis_h_sb", [H, NFAST])
        basis_w = sb("basis_w_sb", [W, 4, MODES])
        ident = sb("ident_m", [MODES, MODES])
        cols = sb("cols", [W, 4, IT, 4, MODES])
        xh = sb("xh", [MODES, NL, IT, MODES])
        col_ps = [ctx.enter_context(nc.psum_tensor(f"col_ps{i}", [W, 4, NFAST], F32)) for i in range(4)]
        xh_ps = [ctx.enter_context(nc.psum_tensor(f"xh_ps{i}", [128, IT, MODES], F32)) for i in range(2)]
        raw_ps = [ctx.enter_context(nc.psum_tensor(f"raw_ps{i}", [CI, MODES // 2, MODES], F32)) for i in range(2)]
        full, pair = pair, pair[0:CI]
        zeros_set = sem("zeros_set")
        raw = pair[:, :, :, 1, :]
        raw_v = raw.rearrange("i (h u) v b -> i h u v b", h=2)
        PIECES = 16
        ops1 = region[:, 0:C * PF].rearrange("p (c o) -> p c o", c=C)
        op1_stored = sem("op1_stored")
        combined, turned = sem("combined"), sem("turned")
        basis_in, w1_in = sem("basis_in"), sem("w1_in")
        x_in = [sem(f"x_in{t}") for t in range(NX_IN)]
        rows_summed = sem("rows_summed")
        cols_act, cols_dve = sem("cols_act"), sem("cols_dve")
        modes_done = sem("modes_done")
        xh_kept = sem("xh_kept")
        raw_done = sem("raw_done")
        raw_kept = sem("raw_kept")
        block = ctx.enter_context(nc.Block())

        @block.sync
        def _(sp):
            sp.dma_start(basis_h[:], a["basis_h"]).then_inc(basis_in, 16)
            sp.dma_start(basis_w[:], a["basis_w"].rearrange("w (k v) -> w k v", k=4)).then_inc(basis_in, 16)
            sp.dma_start(ident[:], a["ident"][0:MODES, 0:MODES]).then_inc(basis_in, 16)
            for b in range(B):
                for t in range(NL):
                    n = b * NL + t
                    sp.wait_ge(rows_summed, 2 * n + 2)
                    sp.dma_start(xin[:, n % NX_IN], a["x"][b, t * IT:(t + 1) * IT].rearrange("i h w -> h i w"))\
                      .then_inc(x_in[n % NX_IN], 16)
                    if NX_IN <= n < NX_IN + PIECES:
                        cs = slice((n - NX_IN) * C // PIECES, (n - NX_IN + 1) * C // PIECES)
                        sp.dma_start(op_d[:, 1, cs].rearrange("p c o -> p (c o)"), ops1[:, cs].rearrange("p c o -> p (c o)"))\
                          .then_inc(op1_stored, 16)
                if b == 4:
                    sp.wait_ge(op1_stored, 16 * PIECES)
                    sp.dma_start(w1[:], a["w1"].rearrange("i o u v -> i o (u v)")).then_inc(w1_in, 16)
            sp.wait_ge(w1_in, 16)

        @block.gpsimd
        def _(pool):
            nc.gpsimd.memset(full[CI:128, :, :, 0, :], 0.0).then_inc(zeros_set, 1)
            pool.wait_ge(zeros_set, 1)

        @block.tensor
        def _(pe):
            pe.sem_inc(rows_summed, 2 * NX_IN)
            pe.sem_inc(modes_done, 2)
            pe.sem_inc(raw_done, 2)
            pe.wait_ge(basis_in, 48)
            with pe.Fori(0, B) as b:
                for half in range(2):
                    for t in range(4 * half, 4 * half + 4):
                        pe.wait_ge(x_in[t % NX_IN], b * (NL // NX_IN * 16) + (t // NX_IN + 1) * 16)
                        for g in range(2):
                            pe.wait_ge((cols_act, cols_dve)[g], b * NL + t + 1)
                            for k in range(4):
                                mm = nc.tensor.matmul(col_ps[2 * (t % 2) + g][:, k, :], xin[:, t % NX_IN, 4 * g + k, :], basis_h[:],
                                                      start=True, stop=True)
                            mm.then_inc(rows_summed, 1)
                    for s in (cols_act, cols_dve):
                        pe.wait_ge(s, b * NL + 4 * half + 6)
                    pe.wait_ge(xh_kept, b * 2 + half + 1)
                    for k in range(4):
                        for t in range(4):
                            mm = nc.tensor.matmul(xh_ps[half][Q * t:Q * t + MODES], basis_w[:, k, :], cols[:, t, :, k, :],
                                                  start=k == 0, stop=k == 3, skip_group_check=True)
                    mm.then_inc(modes_done, 1)
                pe.wait_ge(xh_kept, b * 2 + 4)
                for h in range(2):
                    pe.wait_ge(raw_kept, b * 2 + h + 1)
                    pe.sem_inc(turned, 1)
                    for ul in range(MODES // 2):
                        u = h * (MODES // 2) + ul
                        mm = nc.tensor.transpose(raw_ps[h][:, ul], xh[:, :, :, u].rearrange("v t i -> v (t i)"), ident[:])
                    mm.then_inc(raw_done, 1)

        def copy_cols(copy, eng, b, half, g, kept):
            eng.wait_ge(modes_done, b * 2 + half + 1)
            for t in range(4 * half, 4 * half + 4):
                eng.wait_ge(rows_summed, b * (2 * NL) + 2 * t + g + 1 + 2 * NX_IN)
                copy(cols[:, t % 4, 4 * g:4 * g + 4].rearrange("w i k u -> w i (k u)"),
                     col_ps[2 * (t % 2) + g][:, :, 0:F4]).then_inc(kept, 1)

        @block.scalar
        def _(act):
            act.sem_inc(cols_act, 2)
            act.sem_inc(raw_kept, 2)
            with act.Fori(0, B) as b:
                for half in range(2):
                    copy_cols(nc.scalar.copy, act, b, half, 0, cols_act)
                for h in range(2):
                    act.wait_ge(raw_done, b * 2 + h + 3)
                    dst = raw_v[:, h, :, :, bass.ds(b, 1)].rearrange("i u v b -> i u (v b)")
                    nc.scalar.copy(dst, raw_ps[h][:]).then_inc(raw_kept, 1)

        @block.vector
        def _(dve):
            dve.sem_inc(cols_dve, 2)
            dve.sem_inc(xh_kept, 2)
            with dve.Fori(0, B) as b:
                for half in range(2):
                    copy_cols(nc.vector.tensor_copy, dve, b, half, 1, cols_dve)
                    dve.wait_ge(modes_done, b * 2 + half + 3)
                    if half == 0:
                        dve.wait_ge(raw_done, b * 2 + 2)
                    for t in range(4):
                        last = nc.vector.tensor_copy(xh[:, 4 * half + t], xh_ps[half][Q * t:Q * t + MODES])
                    last.then_inc(xh_kept, 1)
            dve.wait_ge(raw_kept, 2 * B + 2)
            zero, rest, back = slice(0, 1), slice(1, MODES), slice(MODES - 1, 0, -1)
            for u, nu in ((zero, zero), (rest, back)):
                for v, nv in ((zero, zero), (rest, back)):
                    last = nc.vector.tensor_tensor(pair[:, u, v, 0, :], raw[:, nu, nv, :], raw[:, u, v, :], ALU.add)
            last.then_inc(combined, 1)
            dve.wait_ge(combined, 1)
            nc.vector.scalar_tensor_tensor(raw.rearrange("i u v b -> i (u v) b"), raw.rearrange("i u v b -> i (u v) b"), -2.0,
                                           pair[:, :, :, 0, :].rearrange("i u v b -> i (u v) b"), ALU.mult, ALU.add)


def mix(nc, pair, w1):
    with ExitStack() as ctx:
        def sb(name, shape):
            return ctx.enter_context(nc.sbuf_tensor(name, shape, F32))

        def sem(name):
            return ctx.enter_context(nc.semaphore(name))
        w_at = sb("w_at", [CI, 2, MODES, CI])
        sums = sb("sums", [CI, 2, MODES, 2, B])
        mix_ps = [ctx.enter_context(nc.psum_tensor(f"mix_ps{i}", [128, MODES // 2, 2, B], F32)) for i in range(2)]
        at_act, at_dve, sums_ready, mix_begun = map(sem, ("at_act", "at_dve", "sums_ready", "mix_begun"))
        mix_done = sem("mix_done")
        mix_kept = sem("mix_kept")
        block = ctx.enter_context(nc.Block())
        HO = CI // 2

        @block.gpsimd
        def _(pool):
            with pool.Fori(0, MODES // 2) as h:
                for k in range(2):
                    pool.wait_ge(mix_done, 2 * h + k + 1)
                    nc.gpsimd.tensor_copy(sums[:, k].rearrange("i v k b -> i v (k b)"),
                                          pair[:, bass.ds(2 * h + k, 1)].rearrange("i a v k b -> i (a v) (k b)"))\
                      .then_inc(sums_ready, 1)

        @block.scalar
        def _(act):
            with act.Fori(0, MODES // 2) as h:
                for k in range(2):
                    act.wait_ge(mix_done, 2 * h + k + 1)
                    nc.scalar.copy(w_at[:, k, :, 0:HO].rearrange("i v o -> i o v"),
                                   w1[:, 0:HO, bass.ds((2 * h + k) * MODES, MODES)]).then_inc(at_act, 1)

        @block.tensor
        def _(pe):
            pe.sem_inc(mix_done, 2)
            with pe.Fori(0, MODES // 2) as h:
                for k in range(2):
                    pe.wait_ge(at_act, 2 * h + k + 1)
                    pe.wait_ge(at_dve, 2 * h + k + 1)
                    pe.wait_ge(sums_ready, 2 * h + k + 1)
                    pe.wait_ge(mix_kept, 2 * h + k + 1)
                    pe.sem_inc(mix_begun, 1)
                    for v in range(MODES):
                        mm = nc.tensor.matmul(mix_ps[k][(v % 2) * CI:(v % 2 + 1) * CI, v // 2].rearrange("o k b -> o (k b)"),
                                              w_at[:, k, v, :], sums[:, k, v].rearrange("i k b -> i (k b)"),
                                              start=True, stop=True)
                    mm.then_inc(mix_done, 1)

        @block.vector
        def _(dve):
            dve.sem_inc(mix_kept, 2)

            def copy_w(h, k):
                dve.wait_ge(mix_done, 2 * h + k + 1)
                nc.vector.tensor_copy(w_at[:, k, :, HO:CI].rearrange("i v o -> i o v"),
                                      w1[:, HO:CI, bass.ds((2 * h + k) * MODES, MODES)]).then_inc(at_dve, 1)

            def keep(h, k):
                dve.wait_ge(mix_done, 2 * h + k + 3)
                for odd in range(2):
                    last = nc.vector.tensor_copy(
                        pair[:, bass.ds(2 * h + k, 1), odd::2, :, :].rearrange("o a v k b -> o (a v) (k b)"),
                        mix_ps[k][odd * CI:(odd + 1) * CI].rearrange("o v k b -> o v (k b)"))
                last.then_inc(mix_kept, 1)

            copy_w(0, 0)
            copy_w(0, 1)
            with dve.Fori(0, MODES // 2 - 1) as h:
                for k in range(2):
                    keep(h, k)
                    copy_w(h + 1, k)
            keep(MODES // 2 - 1, 0)
            keep(MODES // 2 - 1, 1)
            dve.wait_ge(mix_kept, MODES + 2)
            zero, rest, back = slice(0, 1), slice(1, MODES), slice(MODES - 1, 0, -1)
            for u, nu in ((zero, zero), (rest, back)):
                for v, nv in ((zero, zero), (rest, back)):
                    nc.vector.tensor_tensor(pair[:, u, v, 0, :], pair[:, u, v, 0, :], pair[:, nu, nv, 1, :], ALU.add)


def smooth(nc, a, pair, padded):
    with ExitStack() as ctx:
        def sb(name, shape):
            return ctx.enter_context(nc.sbuf_tensor(name, shape, F32))

        def sem(name):
            return ctx.enter_context(nc.semaphore(name))
        sm_c = sb("sm_c_sb", [128, NFAST])
        ps = [ctx.enter_context(nc.psum_tensor(f"chan_ps{i}", [128, 4, 128], F32)) for i in range(8)]
        smc_in, smc_zero, chan_done, kept_act, kept_dve, padding = map(
            sem, ("smc_in", "smc_zero", "chan_done", "kept_act", "kept_dve", "padding"))
        images = padded.rearrange("m k (b o) -> m k b o", o=CI)
        mixed = pair[:].rearrange("o u v k b -> o (u v) k b")
        block = ctx.enter_context(nc.Block())

        @block.sync
        def _(sp):
            sp.dma_start(sm_c[0:CI, :], a["sm_c"]).then_inc(smc_in, 16)

        @block.gpsimd
        def _(pool):
            nc.gpsimd.memset(sm_c[CI:128, :], 0.0).then_inc(smc_zero, 1)

        @block.tensor
        def _(pe):
            pe.wait_ge(smc_in, 16)
            pe.wait_ge(smc_zero, 1)
            for n in range(4 * KC):
                if n >= 8:
                    pe.wait_ge((kept_act, kept_dve)[n % 2], (n - 8) // 2 + 1)
                for b in range(4):
                    mm = nc.tensor.matmul(ps[n % 8][0:KP, b, 0:NFAST],
                                          mixed[:, (n // 4) * KP:(n // 4 + 1) * KP, 0, 4 * (n % 4) + b],
                                          sm_c[:], start=True, stop=True)
                mm.then_inc(chan_done, 1)

        def keep(copy, eng, kept, n):
            eng.wait_ge(chan_done, n + 1)
            b0 = R + 4 * (n % 4)
            copy(images[:, n // 4, b0:b0 + 4, :], ps[n % 8][0:KP, :, 0:CI]).then_inc(kept, 1)

        @block.scalar
        def _(act):
            for n in range(0, 4 * KC, 2):
                keep(nc.scalar.copy, act, kept_act, n)

        @block.vector
        def _(dve):
            for n in range(1, 4 * KC, 2):
                keep(nc.vector.tensor_copy, dve, kept_dve, n)
            dve.wait_ge(kept_act, 2 * KC)
            dve.wait_ge(kept_dve, 2 * KC)
            for edge, own in ((slice(0, R), R), (slice(B + R, B + 2 * R), B + R - 1)):
                nc.vector.tensor_copy(images[:, :, edge, :],
                                      images[:, :, own, :].unsqueeze(2).broadcast_to([KP, KC, R, CI])).then_inc(padding, 1)
            dve.wait_ge(padding, 2)


def coefs(nc, a, gauss, padded, win_t, bias_f, coef_d):
    NCH = 2 * len(LIVE)
    PIECE = 4 * 2 * PF
    QN = 2
    NY, NC = QN * NCH, 4 * QN * NCH
    STEPS = B // (2 * QN)
    with ExitStack() as ctx:
        def sb(name, shape):
            return ctx.enter_context(nc.sbuf_tensor(name, shape, F32))

        def sem(name):
            return ctx.enter_context(nc.semaphore(name))
        synth = sb("synth_sb", [KP, 2, KC, PIECE])
        now = sb("now", [KP, KC, QN * 128])
        coming = sb("coming", [KP, KC, QN * 128])
        y = sb("y", [128, QN, NCH, PIECE])
        st = [sb(f"coef_st{h}", [128, 128, NS, NJ]) for h in range(CH)]
        y_ps = [ctx.enter_context(nc.psum_tensor(f"y_ps{i}", [128, PIECE], F32)) for i in range(4)]
        c_ps = [ctx.enter_context(nc.psum_tensor(f"c_ps{i}", [128, 4, 128], F32)) for i in range(4)]
        synth_in = [sem(f"synth_in{i}") for i in range(2)]
        stored = [sem(f"coef_stored{i}") for i in range(CH)]
        st_free = [sem(f"st_free{i}") for i in range(CH)]
        smoothed = sem("smoothed")
        now_ready = sem("now_ready")
        y_done = sem("y_done")
        y_kept = sem("y_kept")
        c_done = sem("c_done")
        c_kept = sem("c_kept")
        const_set = sem("const_set")
        block = ctx.enter_context(nc.Block())

        @block.sync
        def _(sp):
            with sp.Fori(0, STEPS) as i:
                for n in range(NCH):
                    sp.wait_ge(y_done, i * NY + QN * (n - 1) + NY)
                    sp.dma_start(synth[:, n % 2], a["synth"][n].rearrange("m (k p) -> m k p", k=KC)).then_inc(synth_in[n % 2], 16)

        @block.gpsimd
        def _(pool):
            with pool.Fori(0, STEPS) as i:
                for e in range(2 * QN):
                    for h in range(CH):
                        pool.wait_ge(c_kept, i * NC + (2 * e + h + 1) * NCH + 4)
                        pool.dma_start(coef_d[bass.ds(2 * QN * i + e, 1), h].rearrange("b p n -> p (b n)"),
                                       st[h][:].rearrange("p c s j -> p (c s j)")).then_inc(stored[h], 16)
                        if (e, h) != (0, 0):
                            pool.wait_ge(stored[1 - h], i * (2 * QN * 16) + (e + h) * 16)
                            pool.sem_inc(st_free[1 - h], 1)
                pool.wait_ge(stored[CH - 1], (i + 1) * (2 * QN * 16))
                pool.sem_inc(st_free[CH - 1], 1)

        @block.tensor
        def _(pe):
            pe.sem_inc(y_done, NY)
            pe.sem_inc(c_done, NC)
            with pe.Fori(0, STEPS) as i:
                pe.wait_ge(now_ready, i + 1)
                for n in range(NCH):
                    pe.wait_ge(synth_in[n % 2], i * 16 * (NCH // 2) + 16 * (n // 2) + 16)
                    for q in range(QN):
                        m = QN * n + q
                        pe.wait_ge(y_kept, i * NY + m + 1)
                        for k in range(KC):
                            mm = nc.tensor.matmul(y_ps[m % 4][:], now[:, k, q * 128:(q + 1) * 128], synth[:, n % 2, k, :],
                                                  start=k == 0, stop=k == KC - 1)
                        mm.then_inc(y_done, 1)
                pe.wait_ge(y_kept, (i + 1) * NY + 4)
                for e in range(2 * QN):
                    for h in range(CH):
                        for n in range(NCH):
                            m = (2 * e + h) * NCH + n
                            pe.wait_ge(c_kept, i * NC + m + 1)
                            for j in range(4):
                                mm = nc.tensor.matmul(c_ps[m % 4][:, j, :], y[:, e // 2, n, j * 128:(j + 1) * 128],
                                                      win_t[:, e % 2, h * 128:(h + 1) * 128], start=True, stop=True)
                            mm.then_inc(c_done, 1)

        @block.scalar
        def _(act):
            act.sem_inc(y_kept, 4)
            with act.Fori(0, STEPS) as i:
                act.wait_ge(y_done, i * NY + NY)
                act.wait_ge(smoothed, (i + 1) * (2 * R + 1))
                nc.scalar.copy(now[:], coming[:]).then_inc(now_ready, 1)
                act.wait_ge(c_done, (i + 1) * NC)
                for m in range(NY):
                    act.wait_ge(y_done, i * NY + m + 1 + NY)
                    nc.scalar.copy(y[:, m % QN, m // QN, :], y_ps[m % 4][:]).then_inc(y_kept, 1)

        @block.vector
        def _(dve):
            def smooth_batch(i, addr):
                for t in range(2 * R + 1):
                    src = padded[:, :, addr(t * CI)]
                    if t == 0:
                        step = nc.vector.tensor_scalar(coming[:], src, gauss[0], None, ALU.mult)
                    else:
                        dve.wait_ge(smoothed, i * (2 * R + 1) + t)
                        step = nc.vector.scalar_tensor_tensor(coming[:], src, gauss[t], coming[:], ALU.mult, ALU.add)
                    step.then_inc(smoothed, 1)

            def keep_coefs(i):
                for e in range(2 * QN):
                    for h in range(CH):
                        dve.wait_ge(st_free[h], 2 * QN * i + e + 1)
                        for n in range(NCH):
                            m = (2 * e + h) * NCH + n
                            dve.wait_ge(c_done, i * NC + m + 1 + NC)
                            j = 4 * (n % 2)
                            nc.vector.tensor_tensor(st[h][:, :, SLOT[n // 2], j:j + 4].rearrange("p c j -> p j c"),
                                                    c_ps[m % 4][:], bias_f[:, h], ALU.add).then_inc(c_kept, 1)

            smooth_batch(0, lambda off: slice(off, off + QN * 128))
            dve.sem_inc(c_kept, 4)
            for h in range(CH):
                dve.sem_inc(st_free[h], 1)
            for h in range(CH):
                for j in range(0, NJ, 4):
                    nc.vector.tensor_copy(st[h][:, :, CONST, j:j + 4].rearrange("p c j -> p j c"), bias_f[:, h])\
                      .then_inc(const_set, 1)
            with dve.Fori(0, STEPS - 1) as i:
                dve.wait_ge(now_ready, i + 1)
                smooth_batch(i + 1, lambda off: bass.ds((i + 1) * (QN * 128) + off, QN * 128))
                keep_coefs(i)
            keep_coefs(STEPS - 1)


def first_row(n):
    return n - P // 2 if n >= P // 2 else n - P // 2 + 2 * P


def product_out(nc, ps, zt, q, wout_t):
    for h in range(CH):
        for e in range(2):
            mm = nc.tensor.matmul(ps[e * CI:(e + 1) * CI, 0:4 * NZ].rearrange("o (x n) -> o x n", x=4),
                                  wout_t[:, h, :], zt[:, h, 4 * q:4 * q + 4, e, :], start=h == 0, stop=h == CH - 1)
    return mm


def place(nc, img, ps, n, q, bout):
    groups = img[:, first_row(n)::2 * P, :].rearrange("p j (g x) -> p x g j", x=4)
    src = ps[:, 0:4 * NZ].rearrange("p (x t j) -> p x t j", x=4, t=NT)
    if q == 0:
        pieces = ((slice(1, 6), groups[:, :, 1:11:2, :]), (slice(6, 11), groups[:, :, 23:32:2, :]))
    else:
        pieces = ((slice(0, 6), groups[:, :, 0:12:2, :]), (slice(6, 10), groups[:, :, 24:32:2, :]))
    for ts, dst in pieces:
        last = nc.vector.tensor_scalar(dst, src[:, :, ts, :], bout[:, 0:1], None, ALU.add)
    return last


def spread_mid(nc, img, mid_out, mid_set):
    for n in range(2 * P):
        nc.gpsimd.tensor_copy(img[:, first_row(n)::2 * P, MID0:MID1],
                              mid_out[:, n].unsqueeze(2).broadcast_to([128, NJ, MID1 - MID0])).then_inc(mid_set, 1)


def conv(nc, a, op_d, coef_d, z_d, mid, mid_out, wout_t, bdw, bout, out):
    NCB = C // CB
    BG = 4
    NG = BI // BG
    PER = CB * NG
    SLOTS = 2 * P
    RUNS = NCB // SLOTS
    HALF = SLOTS // 2 * CB
    NB = 4
    ZB = 4
    ALL_STORED = 32 * NCB + 32
    assert NG == 2 and RUNS == BI // 2 and B == 2 * BI
    places = sorted([(s, 1) for s in range(3, SLOTS)] + [(s, 3) for s in (5, 9, 13)])
    row_at = {place: n for n, place in enumerate(places)}
    with ExitStack() as ctx:
        def sb(name, shape):
            return ctx.enter_context(nc.sbuf_tensor(name, shape, F32))

        def sem(name):
            return ctx.enter_context(nc.semaphore(name))

        def bank(name):
            return ctx.enter_context(nc.psum_tensor(name, [128, 512], F32))
        WORDS = dict(xs=BI * CB * NX, xsh=BI * CB * NS * (NJ + 1), op=2 * CB * PF, z=2 * CB * BI * NZ)
        starts = dict(zip(WORDS, accumulate([2 * words for words in WORDS.values()], initial=0)))
        space = sb("conv_space", [128, 2 * sum(WORDS.values())])

        def part(name, k):
            start = starts[name] + k * WORDS[name]
            return space[:, start:start + WORDS[name]]
        xs = [part("xs", k).rearrange("p (b c n) -> p b c n", b=BI, c=CB) for k in range(2)]
        xsh = [part("xsh", k).rearrange("p (b c s j) -> p b c s j", b=BI, c=CB, s=NS) for k in range(2)]
        op = [part("op", k).rearrange("p (s c o) -> p s c o", s=2, c=CB) for k in range(2)]
        z, z_top = [part("z", k).rearrange("p (k c b t j) -> p k c b t j", k=2, c=CB, b=BI, t=NT) for k in range(2)]
        img2 = space[:, 0:H * W].rearrange("p (h w) -> p h w", h=H)
        ps = [bank(f"z_ps{i}") for i in range(NB)]
        xs_in = [sem(f"xs_in{i}") for i in range(4)]
        stored = [sem(f"z_stored{i}") for i in range(4)]
        z_done = sem("z_done")
        z_act, z_dve = sem("z_act"), sem("z_dve")
        up_done, down_done = sem("up_done"), sem("down_done")
        zero_set = sem("zero_set")
        zt = [sb(f"zt{i}", [128, CH, P, 2, NZ]) for i in range(ZB)]
        img = sb("img", [128, H, W])
        o_ps = [bank(f"out_ps{i}") for i in range(4)]
        z_in = [sem(f"row_in{i}") for i in range(ZB)]
        gelu_done = sem("row_gelu_done")
        o_done = sem("row_done")
        o_kept = sem("row_kept")
        img_stored, img2_stored = sem("img_stored"), sem("img2_stored")
        img_free, img2_free = sem("img_free"), sem("img2_free")
        flat_in, mid_step, mid_act, mid_done, mid_kept, mid_set = map(
            sem, ("flat_in", "mid_step", "mid_gelu", "mid_done", "mid_kept", "mid_spread"))
        z_v = z_d.rearrange("(h c) x b n -> c h x b n", h=CH)
        flat = zt[0][:, 0].rearrange("c x b n -> c (x b n)")[:, 0:CH * 4 * PF]\
            .rearrange("c (h r s x) -> c h r s x", h=CH, r=2, s=2)
        by_role = sb("by_role", [128, CH, 2, P])
        bin_col = sb("bin_col", [128, CH])
        block = ctx.enter_context(nc.Block())

        def channel(i, s, group):
            return (i - group * RUNS) * HALF + s // 2 * CB + s % 2 * 128

        def load_row(eng, i, n):
            eng.wait_ge(o_done, i * (4 * P) + 2 * n + 2)
            for h in range(CH):
                src = z_v[:, h, n % (2 * P) * P:(n % (2 * P) + 1) * P, bass.ds(2 * i + n // (2 * P) * 2, 2)]
                eng.dma_start(zt[n % ZB][:, h], src).then_inc(z_in[n % ZB], 16)

        @block.sync
        def _(sp):
            for r in range(4):
                sp.sem_inc(stored[r], 32)

            def load(i, s, c, group):
                k = s % 2
                first = channel(i, s, group) + c
                b = slice(group * BI, (group + 1) * BI)
                sp.wait_ge(z_done, i * (SLOTS * PER) + s * PER + (c + 2) * NG)
                sp.dma_start(xs[k][:, :, c:c + 2].rearrange("p b c n -> p b (c n)"),
                             coef_d[b, k, :, bass.ds((first - k * 128) * NX, 2 * NX)].rearrange("b p n -> p b n"))\
                  .then_inc(xs_in[2 * k + c // 2], 16)
                sp.dma_start(op[k][:, :, c:c + 2].rearrange("p s c o -> p s (c o)"),
                             op_d[:, :, bass.ds(first, 2)].rearrange("p s c o -> p s (c o)"))\
                  .then_inc(xs_in[2 * k + c // 2], 16)

            def store(i, s, c, group):
                for kept in (z_act, z_dve):
                    sp.wait_ge(kept, i * (SLOTS * CB * 2) + 2 * (s * CB + c + 1) + 2 + NB)
                dst = z_d[bass.ds(channel(i, s, group) + c, 2), :, group * BI:(group + 1) * BI].rearrange("c p b n -> p c (b n)")
                for part, src in ((slice(0, 32), z_top), (slice(32, 128), z)):
                    sp.dma_start(dst[part], src[part, s % 2, c:c + 2].rearrange("p c b t j -> p c (b t j)"))\
                      .then_inc(stored[s % 2 * 2 + c // 2], 16)

            def run(i, group, last):
                for s in range(SLOTS):
                    for c in range(CB):
                        if c % 2:
                            if s + 2 < SLOTS:
                                load(i, s + 2, c - 1, group)
                            elif not last:
                                load(i + 1, s + 2 - SLOTS, c - 1, group)
                            elif group == 0:
                                load(i + 1, s + 2 - SLOTS, c - 1, 1)
                            store(i, s, c - 1, group)

            for s in range(2):
                for c in range(0, CB, 2):
                    load(0, s, c, 0)
            for group in range(2):
                if group == 1:
                    sp.wait_ge(mid_step, CH)
                    for n in range(ZB - 1):
                        load_row(sp, 0, n)
                with sp.Fori(group * RUNS, (group + 1) * RUNS - 1) as i:
                    run(i, group, False)
                run((group + 1) * RUNS - 1, group, True)
                for r in range(4):
                    sp.wait_ge(stored[r], 32 * (group + 1) * (NCB // 2) + 32)
            with sp.Fori(0, RUNS // 2) as i:
                for k in range(2):
                    for n in range(2 * P):
                        load_row(sp, 2 * i + (RUNS + k), n)

        @block.tensor
        def _(pe):
            pe.sem_inc(z_done, 2 * PER)

            def row_out(i, n):
                pe.wait_ge(gelu_done, i * (4 * P) + 2 * n + 2)
                for q in range(2):
                    pe.wait_ge(o_kept, i * (4 * P) + 2 * n + q + 1)
                    product_out(nc, o_ps[(2 * n + q) % 4], zt[n % ZB], q, wout_t).then_inc(o_done, 1)

            def run(i, group):
                for s in range(SLOTS):
                    k = s % 2
                    for c in range(CB):
                        if c % 2 == 0:
                            pe.wait_ge(xs_in[2 * k + c // 2], i * (SLOTS // 2 * 32) + s // 2 * 32 + 32)
                        pe.wait_ge(up_done, i * (SLOTS * CB) + s * CB + c + 1)
                        pe.wait_ge(down_done, i * (SLOTS * CB) + s * CB + c + 1)
                        for g in range(NG):
                            pe.wait_ge((z_act, z_dve)[g], i * (SLOTS * CB * 2) + 2 * (s * CB + c) + 2)
                            tile = ps[(c * NG + g) % NB][:, 0:BG * NT * (NJ + 1)].rearrange("p (b t j) -> p b t j", b=BG, t=NT)
                            bs = slice(g * BG, (g + 1) * BG)
                            nat = xs[k][:, bs, c, :].rearrange("p b (s j) -> p b s j", s=NS)
                            for side, ts in ((0, slice(1, NT)), (1, slice(0, NS))):
                                nc.tensor.matmul(tile[0:PF, :, ts, :], op[k][:, side, c, :], xsh[k][:, bs, c],
                                                 start=side == 0, stop=side == 1, skip_group_check=True)
                                mm = nc.tensor.matmul(tile[PF:128, :, ts, 0:NJ], op[k][:, side, c, :], nat,
                                                      start=side == 0, stop=side == 1, skip_group_check=True)
                            mm.then_inc(z_done, 1)
                        if group == 1 and (s, c) in row_at:
                            row_out(i - RUNS, row_at[s, c])

            with pe.Fori(0, RUNS) as i:
                run(i, 0)
            pe.sem_inc(o_done, 2 * ZB)
            pe.wait_ge(mid_act, CH)
            for e in range(2):
                for h in range(CH):
                    mm = nc.tensor.matmul(o_ps[3][e * CI:(e + 1) * CI, 0:128], wout_t[:, h, :],
                                          mid[:, h].rearrange("c n j -> c (n j)"), start=h == 0, stop=h == CH - 1)
            mm.then_inc(mid_done, 1)
            with pe.Fori(RUNS, 2 * RUNS) as i:
                run(i, 1)
            with pe.Fori(0, RUNS // 2) as i:
                for k in range(2):
                    for n in range(2 * P):
                        row_out(2 * i + (RUNS + k), n)

        def shift(copy, eng, i, s, c, done, up):
            k = s % 2
            if c % 2 == 0:
                eng.wait_ge(xs_in[2 * k + c // 2], i * (SLOTS // 2 * 32) + s // 2 * 32 + 32)
            nat = xs[k][:, :, c, :].rearrange("p b (s j) -> p b s j", s=NS)
            if up:
                copy(xsh[k][0:PF, :, c, :, 1:NJ + 1], nat[PF:128]).then_inc(done, 1)
            else:
                copy(xsh[k][PF:128, :, c, :, 0:NJ], nat[0:PF]).then_inc(done, 1)

        def keep_channel(copy, eng, kept, i, s, c, g):
            if c % 2 == 0:
                eng.wait_ge(stored[s % 2 * 2 + c // 2], i * (SLOTS // 2 * 32) + 32 * (s // 2) + 32)
            tile = ps[(c * NG + g) % NB][:, 0:BG * NT * (NJ + 1)].rearrange("p (b t j) -> p b t j", b=BG, t=NT)
            bs = slice(g * BG, (g + 1) * BG)
            eng.wait_ge(z_done, i * (SLOTS * PER) + s * PER + c * NG + g + 1 + 2 * PER)
            copy(z[:, s % 2, c, bs], tile[:, :, :, 0:NJ]).then_inc(kept, 1)
            copy(z_top[0:32, s % 2, c, bs], tile[0:32, :, :, 1:NJ + 1]).then_inc(kept, 1)

        @block.scalar
        def _(act):
            def gelu(i, n):
                act.wait_ge(z_in[n % ZB], i * (2 * P // ZB * 32) + 32 * (n // ZB) + 32)
                for h in range(CH):
                    v = zt[n % ZB][:, h].rearrange("c x b n -> c (x b n)")
                    nc.scalar.activation(v, v, ACT.Gelu, bias=bdw[:, h:h + 1]).then_inc(gelu_done, 1)

            act.sem_inc(z_act, NB)
            act.wait_ge(zero_set, 4)
            for c in range(CB):
                shift(nc.scalar.copy, act, 0, 0, c, up_done, True)

            def run(i, group, last):
                for s in range(SLOTS):
                    for c in range(CB):
                        if group == 1 and (s, c) in row_at:
                            n = row_at[s, c]
                            gelu(i - RUNS, n)
                            if not (last and n + ZB - 1 >= 2 * P):
                                load_row(act, i - RUNS, n + ZB - 1)
                        keep_channel(nc.scalar.copy, act, z_act, i, s, c, 0)
                        if not (last and s + 1 == SLOTS):
                            shift(nc.scalar.copy, act, i, s + 1, c, up_done, True)

            with act.Fori(0, RUNS) as i:
                run(i, 0, False)
            act.wait_ge(mid_step, 4 * CH + 2)
            for h in range(CH):
                v = mid[:, h].rearrange("c n j -> c (n j)")
                nc.scalar.activation(v, v, ACT.Gelu, bias=bdw[:, h:h + 1]).then_inc(mid_act, 1)
            with act.Fori(RUNS, 2 * RUNS - 1) as i:
                run(i, 1, False)
            run(2 * RUNS - 1, 1, True)
            with act.Fori(0, RUNS // 2) as i:
                for k in range(2):
                    for n in range(2 * P):
                        gelu(2 * i + (RUNS + k), n)

        @block.vector
        def _(dve):
            def keep_row(image, i, n):
                for q in range(2):
                    dve.wait_ge(o_done, i * (4 * P) + 2 * n + q + 1 + 2 * ZB)
                    place(nc, image, o_ps[(2 * n + q) % 4], n, q, bout).then_inc(o_kept, 1)

            dve.sem_inc(z_dve, NB)
            for k in range(2):
                nc.vector.memset(xsh[k][0:PF, :, :, :, 0], 0.0).then_inc(zero_set, 1)
                nc.vector.memset(xsh[k][PF:128, :, :, :, NJ], 0.0).then_inc(zero_set, 1)
            dve.wait_ge(zero_set, 4)
            for c in range(CB):
                shift(nc.vector.tensor_copy, dve, 0, 0, c, down_done, False)

            def run(i, group, last):
                for s in range(SLOTS):
                    for c in range(CB):
                        keep_channel(nc.vector.tensor_copy, dve, z_dve, i, s, c, 1)
                        if not (last and s + 1 == SLOTS):
                            shift(nc.vector.tensor_copy, dve, i, s + 1, c, down_done, False)
                        if group == 1 and (s, c) in row_at:
                            n = row_at[s, c]
                            if n == 0:
                                dve.wait_ge(img_free, i - (RUNS - 1))
                            keep_row(img, i - RUNS, n)

            with dve.Fori(0, RUNS) as i:
                run(i, 0, False)
            dve.wait_ge(mid_done, 1)
            nc.vector.tensor_scalar(mid_out[:].rearrange("p n j -> p (n j)"), o_ps[3][:, 0:128], bout[:, 0:1], None, ALU.add)\
              .then_inc(mid_kept, 1)
            dve.wait_ge(mid_kept, 1)
            dve.sem_inc(o_kept, 4)
            dve.sem_inc(img_free, 1)
            with dve.Fori(RUNS, 2 * RUNS - 1) as i:
                run(i, 1, False)
            run(2 * RUNS - 1, 1, True)
            for t in range(4):
                dve.wait_ge(stored[t], ALL_STORED)
            dve.sem_inc(img2_free, 1)
            with dve.Fori(0, RUNS // 2) as i:
                for k, (image, its_free) in enumerate(((img2, img2_free), (img, img_free))):
                    dve.wait_ge(its_free, i + (1 + k * RUNS))
                    for n in range(2 * P):
                        keep_row(image, 2 * i + (RUNS + k), n)

        @block.gpsimd
        def _(pool):
            for h in range(CH):
                for role in range(2):
                    for side in range(2):
                        pool.dma_start(flat[:, h, role, side], op_d[role * PF, side, h * 128:(h + 1) * 128]).then_inc(flat_in, 16)
            with nc.allow_non_contiguous_dma(reason="256 words, once"):
                pool.dma_start(bin_col[:], a["b_in"].rearrange("(h c) -> c h", h=CH)).then_inc(flat_in, 16)
            pool.wait_ge(flat_in, 16 * (CH * 4 + 1))
            for h in range(CH):
                nc.gpsimd.tensor_tensor(by_role[:, h], flat[:, h, :, 0, ::P], flat[:, h, :, 1, ::P], ALU.add).then_inc(mid_step, 1)
            pool.wait_ge(mid_step, CH)
            for h in range(CH):
                nc.gpsimd.tensor_scalar(by_role[:, h], by_role[:, h], bin_col[:, h:h + 1], float(P), ALU.mult, ALU.mult).then_inc(mid_step, 1)
            pool.wait_ge(mid_step, 2 * CH)

            def both(role, h):
                return by_role[:, h, role].unsqueeze(2).broadcast_to([128, P, NJ])
            for h in range(CH):
                for tile in range(2):
                    nc.gpsimd.tensor_tensor(mid[:, h, tile * P:(tile + 1) * P], both(0, h), both(1, h), ALU.add).then_inc(mid_step, 1)
            pool.wait_ge(mid_step, 4 * CH)
            nc.gpsimd.tensor_copy(mid[:, :, P // 2:P, 0], by_role[:, :, 1, P // 2:P]).then_inc(mid_step, 1)
            nc.gpsimd.tensor_copy(mid[:, :, 0:P // 2, NJ - 1], by_role[:, :, 0, 0:P // 2]).then_inc(mid_step, 1)
            pool.wait_ge(mid_kept, 1)
            spread_mid(nc, img, mid_out, mid_set)
            pool.wait_ge(mid_set, 2 * P)
            def store_pair(i, image, its_stored, nth, its_free):
                pool.wait_ge(o_kept, i * (4 * P) + 4 * P + 4)
                pool.dma_start(out[bass.ds(2 * i, 2)].rearrange("b o h w -> (b o) (h w)"),
                               image.rearrange("p h w -> p (h w)")).then_inc(its_stored, 16)
                pool.wait_ge(its_stored, nth * 16)
                pool.sem_inc(its_free, 1)

            with pool.Fori(0, RUNS) as i:
                store_pair(i, img[:], img_stored, i + 1, img_free)
            for t in range(4):
                pool.wait_ge(stored[t], ALL_STORED)
            spread_mid(nc, img2, mid_out, mid_set)
            pool.wait_ge(mid_set, 4 * P)
            with pool.Fori(0, RUNS // 2) as i:
                store_pair(2 * i + RUNS, img2, img2_stored, i + 1, img2_free)
                store_pair(2 * i + (RUNS + 1), img[:], img_stored, i + (RUNS + 1), img_free)


NAMES = {"x": "x", "w1": "L0_conv_w1", "w_in": "L1_conv_w_in", "b_in": "L1_conv_b_in",
         "fft_filter": "L1_conv_fft_filter", "w_dw": "L1_conv_w_dw", "b_dw": "L1_conv_b_dw",
         "w_out": "L1_conv_w_out", "b_out": "L1_conv_b_out"}


def kernel(**inputs):
    import numpy as np
    import concourse.bacc as bacc
    from concourse.bass_utils import run_bass_kernel_spmd

    nc = bacc.Bacc("TRN2", target_bir_lowering=False, num_devices=1)
    arrays, aps = {}, {}
    tables, gauss = constants()
    given = {k: np.ascontiguousarray(inputs[v]) for k, v in NAMES.items()}
    for k in ("w_in", "w_out"):
        given[k] = given[k].reshape(given[k].shape[:2])
    for k in ("fft_filter", "w_dw"):
        given[k] = given[k].reshape(C, -1)
    for k, v in {**given, **tables}.items():
        arrays[f"in_{k}"] = v
        aps[k] = nc.dram_tensor(f"in_{k}", v.shape, F32, kind="ExternalInput").ap()
    out = nc.dram_tensor("out", (B, CI, H, W), F32, kind="ExternalOutput").ap()
    build(nc, aps, gauss, out)
    r = run_bass_kernel_spmd(nc, [arrays], core_ids=[0])
    return r.results[0]["out"]
```
